# Optimizing a Trainium2 kernel written in Bass

```python
import numpy as np
import jax
import jax.numpy as jnp

def _softmax(x, axis=-1):
    return jax.nn.softmax(x, axis=axis)

def _gelu(x):
    return jax.nn.gelu(x, approximate=True)

def _silu(x):
    return jax.nn.silu(x)

def _sigmoid(x):
    return jax.nn.sigmoid(x)

def _layernorm(x, axis=-1, eps=1e-05):
    m = jnp.mean(x, axis=axis, keepdims=True)
    v = jnp.var(x, axis=axis, keepdims=True)
    return (x - m) / jnp.sqrt(v + eps)

def _scatter_add(tgt, idx, src, axis=0):
    return tgt.at[idx].add(src)

def _segment_sum(src, seg, n):
    return jax.ops.segment_sum(src, seg, n)
kernel_name = 'mk_gnn_ffn_d1_gnn_r8_e10ea5'

def setup_inputs(seed: int=0):
    np.random.seed(seed)
    _w = jnp.asarray

    def _rec_inputs():
        import jax
        import jax.numpy as jnp
        _gk = jax.random.key(seed)
        x = -0.0001126 + 1 * jax.random.normal(jax.random.fold_in(_gk, 1), (3750, 256), jnp.float32)
        src = jax.random.randint(jax.random.fold_in(_gk, 2), (120000,), 0, 3750, jnp.int32)
        dst = jnp.minimum((3750 * jax.random.uniform(jax.random.fold_in(_gk, 3), (120000,)) ** 2.0).astype(jnp.int32), 29999)
        _o = jnp.argsort(dst, stable=True)
        src = src[_o]
        dst = dst[_o]
        edge_type_8 = jax.random.randint(jax.random.fold_in(_gk, 12), (120000,), 0, 8, jnp.int32)
        return (x, src, dst, edge_type_8)
    x, src, dst, edge_type_8 = _rec_inputs()

    def _L0_gnn_setup():
        import jax, jax.numpy as jnp
        import numpy as np
        N_NODES = 3750
        N_EDGES = 60000
        IN_FEAT = 256
        OUT_FEAT = 256
        N_RELS = 8
        N_HEADS = 4
        HEAD_DIM = OUT_FEAT // N_HEADS
        LEAKY_SLOPE = 0.2
        key = jax.random.key(seed)
        ks = jax.random.split(key, 8)
        inputs = jax.random.normal(ks[0], (N_NODES, IN_FEAT), dtype=jnp.float32)
        conv_weights = jax.random.normal(ks[1], (N_RELS, N_HEADS, IN_FEAT, HEAD_DIM), dtype=jnp.float32) * (1.0 / np.sqrt(IN_FEAT))
        attn_l = jax.random.normal(ks[2], (N_RELS, N_HEADS, HEAD_DIM), dtype=jnp.float32) * 0.1
        attn_r = jax.random.normal(ks[3], (N_RELS, N_HEADS, HEAD_DIM), dtype=jnp.float32) * 0.1
        h_bias = jax.random.normal(ks[4], (OUT_FEAT,), dtype=jnp.float32) * 0.02
        edge_src = jax.random.randint(ks[5], (N_EDGES,), 0, N_NODES, dtype=jnp.int32)
        edge_dst = jax.random.randint(ks[6], (N_EDGES,), 0, N_NODES, dtype=jnp.int32)
        edge_type = jax.random.randint(ks[7], (N_EDGES,), 0, N_RELS, dtype=jnp.int32)
        return {'inputs': inputs, 'conv_weights': conv_weights, 'attn_l': attn_l, 'attn_r': attn_r, 'h_bias': h_bias, 'edge_src': edge_src, 'edge_dst': edge_dst, 'edge_type': edge_type}
    _L0_gnn_all = _L0_gnn_setup()
    _L0_gnn_in = {k: v for k, v in _L0_gnn_all.items() if k in ('conv_weights', 'attn_l', 'attn_r', 'h_bias')}
    del _L0_gnn_all

    def _L0_ffn_setup():
        import jax, jax.numpy as jnp
        import numpy as np
        TOP_K = 2
        LN_EPS = 1e-05
        key = jax.random.key(seed)
        ks = jax.random.split(key, 8)
        B, S, D, E, H = (16, 1024, 256, 8, 1024)
        x = jax.random.normal(ks[0], (B, S, D), dtype=jnp.float32)
        Wr = jax.random.normal(ks[1], (D, E), dtype=jnp.float32) * 0.1
        br = jnp.zeros((E,), dtype=jnp.float32)
        ln_g = jnp.ones((E, D), dtype=jnp.float32)
        ln_b = jnp.zeros((E, D), dtype=jnp.float32)
        W1 = jax.random.normal(ks[2], (E, D, H), dtype=jnp.float32) * (1.0 / np.sqrt(D))
        b1 = jnp.zeros((E, H), dtype=jnp.float32)
        W2 = jax.random.normal(ks[3], (E, H, D), dtype=jnp.float32) * (1.0 / np.sqrt(H))
        b2 = jnp.zeros((E, D), dtype=jnp.float32)
        return {'x': x, 'Wr': Wr, 'br': br, 'ln_g': ln_g, 'ln_b': ln_b, 'W1': W1, 'b1': b1, 'W2': W2, 'b2': b2}
    _L0_ffn_all = _L0_ffn_setup()
    _L0_ffn_in = {k: v for k, v in _L0_ffn_all.items() if k in ('Wr', 'br', 'ln_g', 'ln_b', 'W1', 'b1', 'W2', 'b2')}
    del _L0_ffn_all
    return {'x': x, 'src': src, 'dst': dst, 'edge_type_8': edge_type_8, 'L0_gnn_conv_weights': _L0_gnn_in['conv_weights'], 'L0_gnn_attn_l': _L0_gnn_in['attn_l'], 'L0_gnn_attn_r': _L0_gnn_in['attn_r'], 'L0_gnn_h_bias': _L0_gnn_in['h_bias'], 'L0_ffn_Wr': _L0_ffn_in['Wr'], 'L0_ffn_br': _L0_ffn_in['br'], 'L0_ffn_ln_g': _L0_ffn_in['ln_g'], 'L0_ffn_ln_b': _L0_ffn_in['ln_b'], 'L0_ffn_W1': _L0_ffn_in['W1'], 'L0_ffn_b1': _L0_ffn_in['b1'], 'L0_ffn_W2': _L0_ffn_in['W2'], 'L0_ffn_b2': _L0_ffn_in['b2']}

def reference(x, src, dst, edge_type_8, L0_gnn_conv_weights, L0_gnn_attn_l, L0_gnn_attn_r, L0_gnn_h_bias, L0_ffn_Wr, L0_ffn_br, L0_ffn_ln_g, L0_ffn_ln_b, L0_ffn_W1, L0_ffn_b1, L0_ffn_W2, L0_ffn_b2):
    import jax
    import jax.numpy as jnp

    def _L0_gnn_ref(inputs, conv_weights, attn_l, attn_r, h_bias, edge_src, edge_dst, edge_type):
        import jax, jax.numpy as jnp
        import numpy as np
        N_NODES = 3750
        N_EDGES = 60000
        IN_FEAT = 256
        OUT_FEAT = 256
        N_RELS = 8
        N_HEADS = 4
        HEAD_DIM = OUT_FEAT // N_HEADS
        LEAKY_SLOPE = 0.2
        feat_all = jnp.einsum('ni,rhid->rnhd', inputs, conv_weights)
        feat_src_e = feat_all[edge_type, edge_src]
        feat_dst_e = feat_all[edge_type, edge_dst]
        el = jnp.sum(feat_src_e * attn_l[edge_type], axis=-1)
        er = jnp.sum(feat_dst_e * attn_r[edge_type], axis=-1)
        e = jax.nn.leaky_relu(el + er, negative_slope=LEAKY_SLOPE)
        m = jax.ops.segment_max(e, edge_dst, num_segments=N_NODES)
        ex = jnp.exp(e - m[edge_dst])
        denom = jax.ops.segment_sum(ex, edge_dst, num_segments=N_NODES)
        alpha = ex / denom[edge_dst]
        h = jax.ops.segment_sum(alpha[..., None] * feat_src_e, edge_dst, num_segments=N_NODES)
        h = h.reshape(N_NODES, OUT_FEAT) + h_bias
        return h

    def _L0_ffn_ref(x, Wr, br, ln_g, ln_b, W1, b1, W2, b2):
        import jax, jax.numpy as jnp
        import numpy as np
        TOP_K = 2
        LN_EPS = 1e-05
        B, S, D = x.shape
        N = B * S
        xt = x.reshape(N, D)
        logits = xt @ Wr + br
        probs = jax.nn.softmax(logits, axis=-1)
        top_p, top_idx = jax.lax.top_k(probs, TOP_K)
        weights = top_p / top_p.sum(axis=-1, keepdims=True)
        mu = xt.mean(axis=-1, keepdims=True)
        var = ((xt - mu) ** 2).mean(axis=-1, keepdims=True)
        xn = (xt - mu) * jax.lax.rsqrt(var + LN_EPS)
        xe = xn[None, :, :] * ln_g[:, None, :] + ln_b[:, None, :]
        h = jax.nn.gelu(jnp.einsum('end,edh->enh', xe, W1) + b1[:, None, :], approximate=False)
        y = jnp.einsum('enh,ehd->end', h, W2) + b2[:, None, :]
        y_tok = jnp.transpose(y, (1, 0, 2))
        sel = jnp.take_along_axis(y_tok, top_idx[:, :, None], axis=1)
        out = (weights[:, :, None] * sel).sum(axis=1)
        return out.reshape(B, S, D)
    x = x + _L0_gnn_ref(_layernorm(x, axis=-1), L0_gnn_conv_weights, L0_gnn_attn_l, L0_gnn_attn_r, L0_gnn_h_bias, src, dst, edge_type_8)
    x = x + _L0_ffn_ref(_layernorm(x, axis=-1)[None], L0_ffn_Wr, L0_ffn_br, L0_ffn_ln_g, L0_ffn_ln_b, L0_ffn_W1, L0_ffn_b1, L0_ffn_W2, L0_ffn_b2)[0]
    return x

_drawn_inputs = setup_inputs


def setup_inputs(seed=0):
    import zlib

    import numpy as np

    out = dict(_drawn_inputs(seed))
    spreads = {'L0_ffn_br': (0.0, 0.1),
     'L0_ffn_ln_g': (1.0, 0.2),
     'L0_ffn_ln_b': (0.0, 0.1),
     'L0_ffn_b1': (0.0, 0.1),
     'L0_ffn_b2': (0.0, 0.1)}
    factors = {}
    for name, (base, spread) in spreads.items():
        noise = np.random.default_rng([zlib.crc32(name.encode()), seed]).standard_normal(out[name].shape)
        drawn = base * np.exp(spread * noise) if base else spread * noise
        out[name] = jnp.asarray(drawn.astype(out[name].dtype))
    for name, factor in factors.items():
        out[name] = (out[name] * factor).astype(out[name].dtype)
    return out
```

```python
from contextlib import ExitStack

import numpy as np
import concourse.bass as bass
import concourse.mybir as mybir

F32 = mybir.dt.float32
I32 = mybir.dt.int32
U32 = mybir.dt.uint32
ALU = mybir.AluOpType
ACT = mybir.ActivationFunctionType
AX = mybir.AxisListType

P = 128
N_NODES = 3750
N_EDGES = 120000
D = 256
HEADS = 4
HD = D // HEADS
RELS = 8
EXPERTS = 8
HID = 1024
TILES = -(-N_NODES // P)
ROWS = TILES * P
KD = D // P
KH = HID // P

FW = D + HEADS
UNIT = 128
BLK = 4
EBLOCKS = -(-N_EDGES // (BLK * UNIT))
CHUNK_ROWS = EBLOCKS * BLK
PAIRS = EBLOCKS + TILES - 1
GB = 8
GROUPS = PAIRS // GB
GU = GB * BLK
assert GROUPS * GB == PAIRS and GU * HEADS == P
BIG = 1.0e38
EPS = 1e-5
SLOPE = 0.2
LBP = 47
LBJ = EBLOCKS // LBP
assert LBP * LBJ == EBLOCKS

SLOT_TILE = 256
SLOT_TILES = (2 * ROWS + EXPERTS * (SLOT_TILE - 1)) // SLOT_TILE
SLOTS = SLOT_TILES * SLOT_TILE

E_W2 = KD * HID
E_G = E_W2 + KH * D
E_B = E_G + KD
E_B1 = E_B + KD
E_W = E_B1 + KH

C_ID, C_IOTA, C_MASKU, C_SELH, C_IOTA8, C_PAIR, C_CHUNK, C_THR, C_TILE, C_SELHT, C_TRI, C_SLOT = (
    0, 128, 256, 288, 292, 300, 333, 334, 363, 392, 520, 648)
C_W = C_SLOT + SLOT_TILES


def constants():
    c = np.zeros((P, C_W), np.float32)
    p = np.arange(P)
    c[:, C_ID:C_ID + P] = np.eye(P)
    c[:, C_IOTA:C_IOTA + P] = p[None, :]
    c[:, C_MASKU:C_MASKU + GU] = p[:, None] // HEADS == np.arange(GU)[None, :]
    c[:, C_SELH:C_SELH + HEADS] = p[:, None] % HEADS == np.arange(HEADS)[None, :]
    c[:, C_IOTA8:C_IOTA8 + RELS] = np.arange(RELS)[None, :]
    c[:, C_PAIR:C_PAIR + GROUPS] = GB * np.arange(GROUPS)[None, :] + p[:, None] // (HEADS * BLK)
    c[:, C_CHUNK] = p // HEADS % BLK
    c[:, C_THR:C_THR + TILES - 1] = P * (np.arange(TILES - 1)[None, :] + 1)
    c[:, C_TILE:C_TILE + TILES - 1] = np.arange(TILES - 1)[None, :]
    c[:HEADS, C_SELHT:C_SELHT + P] = p[None, :] % HEADS == np.arange(HEADS)[:, None]
    c[:, C_TRI:C_TRI + P] = p[:, None] < p[None, :]
    c[:, C_SLOT:C_SLOT + SLOT_TILES] = SLOT_TILE * np.arange(SLOT_TILES)[None, :]
    return c


class Chain:

    def __init__(self, eng, sem):
        self.eng, self.sem, self.base, self.n = eng, sem, 0, 0

    def start(self, base):
        self.base, self.n = base, 0

    def __call__(self, ins):
        ins.then_inc(self.sem, 1)
        self.n += 1
        self.eng.wait_ge(self.sem, self.base + self.n)


def wait_apart(pool, sem, value, carrier):
    pool.wait_ge(sem, value)
    pool.sem_inc(carrier, 1)


def mean_var(dve, step, stats, mean, var):
    even, odd = stats[:, :, 1], stats[:, :, 4]
    dve.tensor_tensor(mean, even, odd, ALU.subtract)
    step(dve.tensor_tensor(var, stats[:, :, 2], stats[:, :, 5], ALU.add))
    step(dve.scalar_tensor_tensor(mean, mean, 0.25, mean, ALU.mult, ALU.mult))
    step(dve.scalar_tensor_tensor(var, var, 1.0 / D, mean, ALU.mult, ALU.add))
    step(dve.tensor_tensor(mean, even, odd, ALU.add))
    step(dve.tensor_scalar(mean, mean, 0.5, None, ALU.mult))


def node_stage(nc, sb, x, conv, attn_l, attn_r, feats, slots_x, cst_dram):
    with ExitStack() as ctx:
        def t(name, shape, dt=F32):
            return ctx.enter_context(nc.sbuf_tensor(name, shape, dt))

        def sem(name):
            return ctx.enter_context(nc.semaphore(name))

        wext = t("wext", [P, KD, RELS, FW])
        wer = t("wer", [P, KD, RELS, HEADS])
        attn = t("attn", [P, 2, RELS * D])
        prod = t("prod", [P, RELS * D])
        stats = t("stats", [P, TILES, 6])
        mean = t("mean", [P, TILES])
        std = t("std", [P, TILES])
        rstd = t("rstd", [P, TILES])
        eps = t("eps", [P, 1])
        xh = t("xh", [P, 2, D])
        xT = t("xT", [P, 2, KD, P])
        frow = t("frow", [P, 2, RELS, FW])
        psF = ctx.enter_context(nc.psum_tensor("psF", [P, 2, 2, 512], F32))
        psT = ctx.enter_context(nc.psum_tensor("psT", [P, 2, 512], F32))
        psR = ctx.enter_context(nc.psum_tensor("psR", [P, 2, 512], F32))
        cst_in, x_in, w_in, a_in = sem("cst_in"), sem("x_in"), sem("w_in"), sem("a_in")
        v_step = sem("v_step")
        var_ready, std_ready = sem("var_ready"), sem("std_ready")
        w_ready = sem("w_ready")
        acc_zero, slots_zero = sem("acc_zero"), sem("slots_zero")
        xh_ready, xT_ready, xT_copied = sem("xh_ready"), sem("xT_ready"), sem("xT_copied")
        er_ready, er_copied = sem("er_ready"), sem("er_copied")
        pair_ready = [sem("pair_ready_act"), sem("pair_ready_dve")]
        pair_copied = [sem("pair_copied_act"), sem("pair_copied_dve")]
        row_stored = [sem("row_stored0"), sem("row_stored1")]
        xs, er_sb, cst, acc = sb["xs"], sb["er"], sb["cst"], sb["acc"]
        ident = cst[:, C_ID:C_ID + P]
        feats_tiles = feats.rearrange("(n r) w -> n (r w)", r=RELS)

        with nc.Block() as block:
            @block.sync
            def _(sp):
                sp.dma_start(cst[:], cst_dram).then_inc(cst_in, 16)
                sp.dma_start(xs[:], x.rearrange("(t p) f -> p t f", p=P)).then_inc(x_in, 16)
                for k in range(KD):
                    for r in range(RELS):
                        sp.dma_start(wext[:, k, r, 0:D], conv[k * P:(k + 1) * P, r * D:(r + 1) * D]).then_inc(w_in, 16)
                for a, src in enumerate((attn_l, attn_r)):
                    sp.dma_start(attn[:, a, :], src.to_broadcast([P, RELS * D])).then_inc(a_in, 16)
                sp.wait_ge(acc_zero, 1)
                for k in range(SLOTS // P):
                    sp.dma_start(slots_x[k * P:(k + 1) * P, :], acc[:, 0, 0:D]).then_inc(slots_zero, 16)
                sp.sem_inc(row_stored[0], 16)
                sp.sem_inc(row_stored[1], 16)
                with sp.Fori(0, TILES // 2) as i:
                    for q in range(2):
                        sp.wait_ge(pair_copied[0], i * 4 + 2 * q + 3)
                        sp.wait_ge(pair_copied[1], i * 4 + 2 * q + 3)
                        sp.dma_start(feats_tiles[bass.ds(i * 256 + q * P, P), :],
                                     frow[:, q].rearrange("p r w -> p (r w)")).then_inc(row_stored[q], 16)
                for q in range(2):
                    sp.wait_ge(row_stored[q], 16 * (TILES // 2 + 1))
                sp.wait_ge(slots_zero, 16 * (SLOTS // P))

            @block.vector
            def _(dve):
                step = Chain(dve, v_step)
                dve.sem_inc(pair_copied[1], 1)
                dve.sem_inc(er_copied, 2)
                dve.memset(acc[:], 0.0).then_inc(acc_zero, 1)
                step(dve.memset(eps[:], EPS))
                dve.wait_ge(x_in, 16)
                with dve.Fori(0, TILES) as i:
                    dve.bn_stats(stats[:, bass.ds(i, 1), :].rearrange("p a c -> p (a c)"),
                                 xs[:, bass.ds(i, 1), :].rearrange("p a f -> p (a f)")).then_inc(v_step, 1)
                dve.wait_ge(v_step, step.n + TILES)
                step.start(step.n + TILES)
                mean_var(dve, step, stats, mean[:], std[:])
                dve.sem_inc(var_ready, 1)
                dve.wait_ge(std_ready, 1)
                step(dve.reciprocal(rstd[:], std[:]))

                def normalise(t_, q):
                    at = bass.ds(t_, 1)
                    dve.tensor_scalar(xh[:, q], xs[:, at, :].rearrange("p a f -> p (a f)"), mean[:, at], rstd[:, at],
                                      ALU.subtract, ALU.mult).then_inc(xh_ready, 1)

                normalise(0, 0)
                normalise(1, 1)
                dve.wait_ge(w_in, 16 * KD * RELS)
                dve.wait_ge(a_in, 32)
                for k in range(KD):
                    for a in range(2):
                        step(dve.tensor_tensor(prod[:].rearrange("p (r c) -> p r c", r=RELS), wext[:, k, :, 0:D],
                                               attn[:, a, :].rearrange("p (r c) -> p r c", r=RELS), ALU.mult))
                        dst = wext[:, k, :, D:FW] if a == 0 else wer[:, k]
                        step(dve.tensor_reduce(dst, prod[:].rearrange("p (r h d) -> p r h d", r=RELS, h=HEADS),
                                               AX.X, ALU.add))
                dve.sem_inc(w_ready, 1)

                def finish(i, q, ahead):
                    dve.wait_ge(er_ready, i * 2 + q + 1)
                    dve.tensor_copy(er_sb[:, bass.ds(i * 2 + q, 1), :].rearrange("p a c -> p (a c)"),
                                    psR[:, q, 0:RELS * HEADS]).then_inc(er_copied, 1)
                    dve.wait_ge(row_stored[q], i * 16 + 16)
                    for pair in (1, 3):
                        dve.wait_ge(pair_ready[1], i * 4 + 2 * q + pair // 2 + 1)
                        dve.tensor_copy(frow[:, q, 2 * pair:2 * pair + 2], psF[:, 1, :, 0:FW]).then_inc(pair_copied[1], 1)
                    if ahead:
                        dve.wait_ge(xT_ready, i * 2 + q + 1)
                        normalise(i * 2 + q + 2, q)

                with dve.Fori(0, TILES // 2 - 1) as i:
                    finish(i, 0, True)
                    finish(i, 1, True)
                for q in range(2):
                    finish(TILES // 2 - 1, q, False)

            @block.scalar
            def _(act):
                act.sem_inc(pair_copied[0], 1)
                act.wait_ge(var_ready, 1)
                act.activation(std[:], std[:], ACT.Sqrt, bias=eps[:]).then_inc(std_ready, 1)
                with act.Fori(0, TILES // 2) as i:
                    for q in range(2):
                        act.wait_ge(xT_ready, i * 2 + q + 1)
                        act.copy(xT[:, q].rearrange("p k c -> p (k c)"), psT[:, q, 0:D]).then_inc(xT_copied, 1)
                        act.wait_ge(row_stored[q], i * 16 + 16)
                        for pair in (0, 2):
                            act.wait_ge(pair_ready[0], i * 4 + 2 * q + pair // 2 + 1)
                            act.copy(frow[:, q, 2 * pair:2 * pair + 2], psF[:, 0, :, 0:FW]).then_inc(pair_copied[0], 1)

            @block.tensor
            def _(pe):
                pe.wait_ge(cst_in, 16)

                def turn(i, q):
                    pe.wait_ge(xh_ready, i * 2 + q + 1)
                    for k in range(KD):
                        ins = pe.transpose(psT[:, q, k * P:(k + 1) * P], xh[:, q, k * P:(k + 1) * P], ident)
                    ins.then_inc(xT_ready, 1)

                def multiply(i, q):
                    pe.wait_ge(xT_copied, i * 2 + q + 1)
                    pe.wait_ge(er_copied, i * 2 + q + 1)
                    for k in range(KD):
                        ins = pe.matmul(psR[:, q, 0:RELS * HEADS], xT[:, q, k], wer[:, k].rearrange("p r h -> p (r h)"),
                                        start=k == 0, stop=k == KD - 1)
                    ins.then_inc(er_ready, 1)
                    for pair in range(4):
                        pe.wait_ge(pair_copied[pair % 2], i * 4 + 2 * q + pair // 2 + 1)
                        for j in range(2):
                            for k in range(KD):
                                ins = pe.matmul(psF[:, pair % 2, j, 0:FW], xT[:, q, k], wext[:, k, 2 * pair + j],
                                                start=k == 0, stop=k == KD - 1)
                        ins.then_inc(pair_ready[pair % 2], 1)

                turn(0, 0)
                pe.wait_ge(w_ready, 1)
                with pe.Fori(0, TILES // 2 - 1) as i:
                    turn(i, 1)
                    multiply(i, 0)
                    turn(i + 1, 0)
                    multiply(i, 1)
                turn(TILES // 2 - 1, 1)
                multiply(TILES // 2 - 1, 0)
                multiply(TILES // 2 - 1, 1)


def schedule_stage(nc, sb, edges):
    with ExitStack() as ctx:
        def t(name, shape, dt=F32):
            return ctx.enter_context(nc.sbuf_tensor(name, shape, dt))

        cst = sb["cst"]
        last_i = t("last_i", [LBP, LBJ, 1], I32)
        last_f = t("last_f", [LBP, LBJ])
        below = t("below", [LBP, LBJ, TILES - 1])
        belows = t("belows", [LBP, TILES - 1])
        ones = t("ones", [LBP, P])
        stairs = t("stairs", [P, TILES - 1])
        passed = t("passed", [P, GROUPS, TILES - 1])
        row = t("row", [P, GROUPS])
        reg_passed = t("reg_passed", [1, GROUPS, TILES - 1])
        pair_row = t("pair_row", [1, GROUPS, 1])
        reg_d = t("reg_d", [1, GROUPS])
        ps = ctx.enter_context(nc.psum_tensor("psC", [P, 512], F32))
        last_in = ctx.enter_context(nc.semaphore("last_in"))
        v_step = ctx.enter_context(nc.semaphore("v_step_schedule"))
        counted = ctx.enter_context(nc.semaphore("counted"))
        steps = TILES - 1
        last_of = edges.rearrange("(p j k) c e -> p j k c e", j=LBJ, k=BLK)[:, :, BLK - 1, 0, UNIT - 1:UNIT]

        with nc.Block() as block:
            @block.sync
            def _(sp):
                with nc.allow_non_contiguous_dma("one word of each edge block"):
                    sp.dma_start(last_i[:], last_of).then_inc(last_in, 16)

            @block.tensor
            def _(pe):
                pe.wait_ge(v_step, 4)
                pe.matmul(ps[:, 0:steps], ones[:], belows[:], start=True, stop=True).then_inc(counted, 1)

            @block.vector
            def _(dve):
                step = Chain(dve, v_step)
                step(dve.memset(ones[:], 1.0))
                dve.wait_ge(last_in, 16)
                step(dve.tensor_copy(last_f[:], last_i[:].rearrange("p j o -> p (j o)")))
                step(dve.tensor_tensor(below[:], last_f[:].unsqueeze(2).to_broadcast([LBP, LBJ, steps]),
                                       cst[0:LBP, C_THR:C_THR + steps].unsqueeze(1).to_broadcast([LBP, LBJ, steps]),
                                       ALU.is_lt))
                step(dve.tensor_reduce(belows[:], below[:].rearrange("p j d -> p d j"), AX.X, ALU.add))
                dve.wait_ge(counted, 1)
                step(dve.tensor_tensor(stairs[:], ps[:, 0:steps], cst[:, C_TILE:C_TILE + steps], ALU.add))
                pair = cst[:, C_PAIR:C_PAIR + GROUPS]
                step(dve.tensor_tensor(passed[:], stairs[:].unsqueeze(1).to_broadcast([P, GROUPS, steps]),
                                       pair.unsqueeze(2).to_broadcast([P, GROUPS, steps]), ALU.is_lt))
                step(dve.tensor_reduce(sb["tile_of"][:], passed[:], AX.X, ALU.add))
                step(dve.tensor_tensor(row[:], pair, sb["tile_of"][:], ALU.subtract))
                step(dve.tensor_scalar(row[:], row[:], float(BLK), cst[:, C_CHUNK:C_CHUNK + 1], ALU.mult, ALU.add))
                step(dve.tensor_copy(sb["row_of"][:], row[:]))
                for b in range(GB):
                    step(dve.tensor_scalar(reg_d[:], pair[0:1, :], float(b), None, ALU.add))
                    step(dve.tensor_tensor(reg_passed[:], stairs[0:1, :].unsqueeze(1).to_broadcast([1, GROUPS, steps]),
                                           reg_d[:].unsqueeze(2).to_broadcast([1, GROUPS, steps]), ALU.is_lt))
                    step(dve.tensor_reduce(pair_row[:].rearrange("p g o -> p (g o)"), reg_passed[:], AX.X, ALU.add))
                    step(dve.tensor_copy(sb["pair_tile"][:, :, b], pair_row[:].rearrange("p g o -> p (g o)")))


def edge_stage(nc, sb, edges, feats):
    with ExitStack() as ctx:
        def t(name, shape, dt=F32):
            return ctx.enter_context(nc.sbuf_tensor(name, shape, dt))

        def psum(name, shape):
            return ctx.enter_context(nc.psum_tensor(name, shape, F32))

        def sem(name):
            return ctx.enter_context(nc.semaphore(name))

        cst, acc, er_sb, pair_tile = sb["cst"], sb["acc"], sb["er"], sb["pair_tile"]
        ident = cst[:, C_ID:C_ID + P]
        iota = cst[:, C_IOTA:C_IOTA + P]
        masku = cst[:, C_MASKU:C_MASKU + GU]
        selh = cst[:, C_SELH:C_SELH + HEADS]
        selht = cst[0:HEADS, C_SELHT:C_SELHT + P]
        iota8 = cst[:, C_IOTA8:C_IOTA8 + RELS]
        row_col = t("row_col", [P, 2], I32)
        meta = t("meta", [P, 2, 3 * UNIT], I32)
        tile_col = t("tile_col", [P, 2])
        rows = t("rows", [P, 3, UNIT])
        reset = t("reset", [P, 2, UNIT + 1])
        cat = t("cat", [P, 2, 5])
        idxT = t("idxT", [P, 2, GU], I32)
        dlT = t("dlT", [P, 2, GU])
        typeT = t("typeT", [P, 2, GU, RELS])
        gath = t("gath", [P, 2, GU, FW])
        hot = t("hot", [P, 2, GU, P])
        hotT = t("hotT", [P, 2, BLK * P])
        er_all = t("er_all", [P, GU * RELS * HEADS])
        er_e = t("er_e", [P, GU, HEADS])
        e_sb = t("e_sb", [P, 2, P])
        seg = t("seg", [P, 2, UNIT])
        dn = t("dn", [P, UNIT])
        spread = t("spread", [P, 5, GU])
        lv = t("lv", [HEADS, 8, GU + 1])
        yz = t("yz", [HEADS, 2, GU])
        first_hot = t("first_hot", [HEADS, P])
        phi_log = t("phi_log", [HEADS, 1])
        phi_diag = t("phi_diag", [HEADS, HEADS])
        yz_all = t("yz_all", [P, 2, GU])
        yz_col = t("yz_col", [P, 2])
        phi = t("phi", [P, HEADS])
        psM = psum("psM", [P, 512])
        psOT = psum("psOT", [P, 2, 512])
        psE = psum("psE", [P, 2, 512])
        psS = psum("psS", [P, 512])
        psP = psum("psP", [P, 2, 512])
        S_ET, S_LV, S_YZ, S_PHI, S_DT = 0, 128, 288, 352, 356

        meta_in = [sem("meta_in0"), sem("meta_in1")]
        gath_in = [sem("gath_in0"), sem("gath_in1")]
        col_ready, rows_ready, rowsT_ready, idx_ready = sem("col_ready"), sem("rows_ready"), sem("rowsT_ready"), sem("idx_ready")
        hot_ready, hotT_ready, hotT_copied, er_done = sem("hot_ready"), sem("hotT_ready"), sem("hotT_copied"), sem("er_done")
        e_ready, eT_ready, spread_ready, lv_ready = sem("e_ready"), sem("eT_ready"), sem("spread_ready"), sem("lv_ready")
        yz_ready, yzT_ready, dn_ready, dnT_ready = sem("yz_ready"), sem("yzT_ready"), sem("dn_ready"), sem("dnT_ready")
        exp_ready, scaled, sum_ready, sum_used = sem("exp_ready"), sem("scaled"), sem("sum_ready"), sem("sum_used")
        v_step = sem("v_step_edges")
        carrier = sem("carrier")
        edge_rows = edges.rearrange("t c e -> t (c e)")

        def each_group(eng, body, first=0):
            loops = (GROUPS - 1 - first) // 2
            with eng.Fori(0, loops) as i:
                for k in range(2):
                    body(i * 2 + (first + k), (first + k) % 2, False)
            for g in range(first + 2 * loops, GROUPS):
                body(g, g % 2, g == GROUPS - 1)

        with nc.Block() as block:
            @block.gpsimd
            def _(pool):
                def gather_meta(g, q):
                    pool.tensor_copy(row_col[:, q:q + 1], sb["row_of"][:, bass.ds(g, 1)]).then_inc(col_ready, 1)
                    wait_apart(pool, col_ready, g + 1, carrier)
                    pool.indirect_dma_start(meta[:, q], None, edge_rows,
                                            bass.IndirectOffsetOnAxis(ap=row_col[:, q:q + 1], axis=0)).then_inc(meta_in[q], 16)

                def gather_features(g, q):
                    wait_apart(pool, idx_ready, g + 1, carrier)
                    for u in range(GU):
                        pool.indirect_dma_start(gath[:, q, u], None, feats,
                                                bass.IndirectOffsetOnAxis(ap=idxT[:, q, u:u + 1], axis=0)).then_inc(gath_in[q], 16)

                gather_meta(0, 0)
                gather_meta(1, 1)
                gather_features(0, 0)
                pool.wait_ge(idx_ready, 1)
                gather_meta(2, 0)
                gather_features(1, 1)

                def group(g, q, last):
                    if not last:
                        pool.wait_ge(idx_ready, g)
                        gather_meta(g + 1, 1 - q)
                    pool.wait_ge(sum_ready, g * GB - GB)
                    gather_features(g, q)

                each_group(pool, group, first=2)

            @block.vector
            def _(dve):
                step = Chain(dve, v_step)
                KM, KG = 7, 37

                def meta_rows(g, q):
                    tiles = sb["tile_of"][:, bass.ds(g, 1)]
                    dve.tensor_copy(tile_col[:, 0:1], tiles)
                    step(dve.tensor_scalar(tile_col[:, 1:2], tiles, -float(P), None, ALU.mult))
                    dve.wait_ge(meta_in[q], 8 * g + 16 - 8 * q)
                    dst, src, typ = (meta[:, q, k * UNIT:(k + 1) * UNIT] for k in range(3))
                    dve.scalar_tensor_tensor(rows[:, 0], src, float(RELS), typ, ALU.mult, ALU.add)
                    dve.tensor_copy(rows[:, 2], typ)
                    step(dve.tensor_scalar(rows[:, 1], dst, tile_col[:, 1:2], None, ALU.add))
                    dve.sem_inc(rows_ready, 1)
                    dve.tensor_scalar(cat[:, q, 2:4], rows[:, 1, 0:UNIT:UNIT - 1], 64.0, tile_col[:, 0:1], ALU.mult, ALU.add)
                    dve.tensor_copy(cat[:, q, 4:5], rows[:, 1, 0:1])
                    dve.memset(reset[:, q, 0:UNIT + 1:UNIT], 0.0)
                    step(dve.tensor_tensor(reset[:, q, 1:UNIT], rows[:, 1, 1:UNIT], rows[:, 1, 0:UNIT - 1], ALU.not_equal))
                    step(dve.tensor_scalar(reset[:, q, 1:UNIT], reset[:, q, 1:UNIT], -BIG, None, ALU.mult))
                    dve.wait_ge(rowsT_ready, g + 1)
                    step(dve.tensor_copy(idxT[:, q], psM[:, 0:P:HEADS]))
                    dve.sem_inc(idx_ready, 1)
                    step(dve.tensor_copy(dlT[:, q], psM[:, P:2 * P:HEADS]))
                    step(dve.tensor_tensor(typeT[:, q], psM[:, 2 * P:3 * P:HEADS].unsqueeze(2).to_broadcast([P, GU, RELS]),
                                           iota8.unsqueeze(1).to_broadcast([P, GU, RELS]), ALU.is_equal))

                def logits(g, q):
                    for b in range(GB):
                        dve.tensor_tensor(hot[:, q, b * BLK:(b + 1) * BLK],
                                          iota.unsqueeze(1).to_broadcast([P, BLK, P]),
                                          dlT[:, q, b * BLK:(b + 1) * BLK].unsqueeze(2).to_broadcast([P, BLK, P]),
                                          ALU.is_equal).then_inc(hot_ready, 1)
                    dve.wait_ge(er_done, GB * g + GB)
                    all4 = er_all[:].rearrange("p (u r h) -> p u r h", u=GU, r=RELS)
                    step(dve.tensor_tensor(all4, psE[:].rearrange("p b (u r h) -> p (b u) r h", r=RELS, h=HEADS),
                                           typeT[:, q].unsqueeze(3).to_broadcast([P, GU, RELS, HEADS]), ALU.mult))
                    step(dve.tensor_reduce(er_e[:], all4.rearrange("p u r h -> p u h r"), AX.X, ALU.add))
                    dve.wait_ge(gath_in[q], 256 * g + 512 - 256 * q)
                    e0 = e_sb[:, 0].rearrange("p (u h) -> p u h", h=HEADS)
                    step(dve.tensor_tensor(e0, gath[:, q, :, D:FW], er_e[:], ALU.add))
                    dve.scalar_tensor_tensor(e_sb[:, 1], e_sb[:, 0], SLOPE, e_sb[:, 0], ALU.mult, ALU.max).then_inc(e_ready, 1)

                def maxima(g, q):
                    fwd, bwd = reset[:, q, 0:UNIT], reset[:, q, UNIT:0:-1]
                    dve.wait_ge(eT_ready, g + 1)
                    step(dve.tensor_tensor_scan(seg[:, 0], fwd, psS[:, S_ET:S_ET + UNIT], -BIG, ALU.add, ALU.max))
                    step(dve.tensor_tensor_scan(seg[:, 1, ::-1], bwd, seg[:, 0, ::-1], -BIG, ALU.add, ALU.max))
                    step(dve.tensor_copy(cat[:, q, 0:2], seg[:, 1, 0:UNIT:UNIT - 1]))
                    dve.tensor_tensor(spread[:], cat[:, q].unsqueeze(2).to_broadcast([P, 5, GU]),
                                      masku.unsqueeze(1).to_broadcast([P, 5, GU]), ALU.mult).then_inc(spread_ready, 1)
                    lf, ll, kf, kl, fp = (psS[0:HEADS, S_LV + k * GU:S_LV + (k + 1) * GU] for k in range(5))
                    k_last, r_last = lv[:, 0], lv[:, 1]
                    go_on, no_go, single, both, m_first, tail = (lv[:, k] for k in range(2, 8))
                    dve.wait_ge(lv_ready, g + 1)
                    step(dve.tensor_copy(k_last[:, 1:GU + 1], kl))
                    step(dve.tensor_tensor(go_on[:, 0:GU], kf, k_last[:, 0:GU], ALU.is_equal))
                    dve.tensor_tensor(single[:, 0:GU], kf, k_last[:, 1:GU + 1], ALU.is_equal)
                    step(dve.tensor_scalar(no_go[:, 0:GU], go_on[:, 0:GU], 1.0, BIG, ALU.subtract, ALU.mult))
                    step(dve.tensor_scalar(single[:, 0:GU], single[:, 0:GU], 1.0, BIG, ALU.subtract, ALU.mult))
                    step(dve.tensor_tensor(both[:, 0:GU], no_go[:, 0:GU], single[:, 0:GU], ALU.min))
                    step(dve.tensor_tensor_scan(r_last[:, 1:GU + 1], both[:, 0:GU], ll, r_last[:, 0:1], ALU.add, ALU.max))
                    step(dve.tensor_tensor(m_first[:, 0:GU], r_last[:, 0:GU], no_go[:, 0:GU], ALU.add))
                    step(dve.tensor_tensor(m_first[:, 0:GU], m_first[:, 0:GU], lf, ALU.max))
                    dve.tensor_copy(tail[:, GU - 1:GU], r_last[:, GU:GU + 1])
                    step(dve.tensor_tensor(tail[:, 0:GU - 1], m_first[:, 1:GU], no_go[:, 1:GU], ALU.add))
                    step(dve.tensor_tensor(tail[:, 0:GU - 1], tail[:, 0:GU - 1], r_last[:, 1:GU], ALU.max))
                    step(dve.tensor_tensor_scan(yz[:, 1, ::-1], both[:, GU:0:-1], tail[:, GU - 1::-1], -BIG, ALU.add, ALU.max))
                    step(dve.tensor_tensor(yz[:, 0], yz[:, 1], single[:, 0:GU], ALU.add))
                    step(dve.tensor_tensor(yz[:, 0], yz[:, 0], m_first[:, 0:GU], ALU.max))
                    step(dve.tensor_tensor(phi_log[:], r_last[:, 0:1], yz[:, 0, 0:1], ALU.subtract))
                    dve.tensor_scalar(first_hot[:], iota[0:HEADS, :], fp[:, 0:1], None, ALU.is_equal)
                    step(dve.tensor_tensor(phi_log[:], phi_log[:], go_on[:, 0:1], ALU.mult))
                    step(dve.tensor_scalar(phi_diag[:], ident[0:HEADS, 0:HEADS], phi_log[:], None, ALU.mult))
                    dve.sem_inc(yz_ready, 1)
                    dve.tensor_copy(k_last[:, 0:1], k_last[:, GU:GU + 1])
                    step(dve.tensor_copy(r_last[:, 0:1], r_last[:, GU:GU + 1]))
                    dve.wait_ge(yzT_ready, g + 1)
                    step(dve.tensor_tensor(yz_all[:], psS[:, S_YZ:S_YZ + 2 * GU].rearrange("p (y u) -> p y u", y=2),
                                           masku.unsqueeze(1).to_broadcast([P, 2, GU]), ALU.mult))
                    step(dve.tensor_reduce(yz_col[:], yz_all[:], AX.X, ALU.add))
                    step(dve.tensor_tensor_scan(seg[:, 0], fwd, seg[:, 1], yz_col[:, 0:1], ALU.add, ALU.max))
                    step(dve.tensor_tensor_scan(seg[:, 1, ::-1], bwd, seg[:, 0, ::-1], yz_col[:, 1:2], ALU.add, ALU.max))
                    step(dve.tensor_tensor(dn[:], psS[:, S_ET:S_ET + UNIT], seg[:, 1], ALU.subtract))
                    dve.sem_inc(dn_ready, 1)

                def sums(g, q):
                    def tile_acc(b, lo, hi):
                        d = dve.value_load(pair_tile[0:1, bass.ds(g, 1), b], min_val=0, max_val=TILES - 1)
                        return acc[:, bass.ds(d, 1), :].rearrange("p a w -> p (a w)")

                    def scale(b):
                        rows_b = gath[:, q, b * BLK:(b + 1) * BLK]
                        feat = rows_b[:, :, 0:D].rearrange("p u (h d) -> p u h d", h=HEADS)
                        dve.tensor_tensor(feat, feat, rows_b[:, :, D:FW].unsqueeze(3).to_broadcast([P, BLK, HEADS, HD]),
                                          ALU.mult).then_inc(scaled, 1)

                    first = tile_acc(0, 0, FW)
                    dve.wait_ge(exp_ready, g + 1)
                    scale(0)
                    dve.tensor_tensor(first[:, D:FW], first[:, D:FW], phi[:], ALU.mult)
                    feat = first[:, 0:D].rearrange("p (h d) -> p h d", h=HEADS)
                    step(dve.tensor_tensor(feat, feat, phi[:].unsqueeze(2).to_broadcast([P, HEADS, HD]), ALU.mult))
                    for b in range(GB):
                        if b + 1 < GB:
                            scale(b + 1)
                        into = tile_acc(b, 0, FW)
                        dve.wait_ge(sum_ready, GB * g + b + 1)
                        step(dve.tensor_tensor(into, into, psP[:, b % 2, 0:FW], ALU.add))
                        dve.sem_inc(sum_used, 1)

                dve.sem_inc(sum_used, 2)
                dve.memset(lv[:, 0, 0:1], -1.0)
                step(dve.memset(lv[:, 1, 0:1], -BIG))
                step(dve.memset(lv[:, 5, GU:GU + 1], 0.0))
                meta_rows(0, 0)
                fixed = step.n

                def group(g, q, last):
                    step.start(g * (KM + KG) + fixed)
                    if not last:
                        meta_rows(g + 1, 1 - q)
                        assert step.n == KM, step.n
                    logits(g, q)
                    maxima(g, q)
                    sums(g, q)
                    assert last or step.n == KM + KG, step.n - KM

                each_group(dve, group)

            @block.scalar
            def _(act):
                def group(g, q, last):
                    for b in range(GB):
                        act.wait_ge(hotT_ready, GB * g + b + 1)
                        act.copy(hotT[:, b % 2], psOT[:, b % 2]).then_inc(hotT_copied, 1)
                    act.wait_ge(dnT_ready, g + 1)
                    act.activation(phi[:], psS[:, S_PHI:S_PHI + HEADS], ACT.Exp)
                    act.activation(gath[:, q, :, D:FW], psS[:, S_DT:S_DT + P].rearrange("p (u h) -> p u h", h=HEADS),
                                   ACT.Exp).then_inc(exp_ready, 1)

                each_group(act, group)

            @block.tensor
            def _(pe):
                def meta_rows(g):
                    pe.wait_ge(rows_ready, g + 1)
                    for k in range(3):
                        ins = pe.transpose(psM[:, k * P:(k + 1) * P], rows[:, k], ident)
                    ins.then_inc(rowsT_ready, 1)

                def turn(g, q, b):
                    pe.wait_ge(hot_ready, GB * g + b + 1)
                    for k in range(BLK):
                        ins = pe.transpose(psOT[:, b % 2, k * P:(k + 1) * P], hot[:, q, b * BLK + k], ident)
                    ins.then_inc(hotT_ready, 1)

                def right_logits(g, b):
                    d = pe.value_load(pair_tile[0:1, bass.ds(g, 1), b], min_val=0, max_val=TILES - 1)
                    table = er_sb[:, bass.ds(d, 1), :].rearrange("p a c -> p (a c)")
                    pe.wait_ge(hotT_copied, GB * g + b + 1)
                    W = RELS * HEADS
                    for k in range(BLK):
                        at = ((b * BLK + k) * W) % 512
                        ins = pe.matmul(psE[:, b // 4, at:at + W], hotT[:, b % 2, k * P:(k + 1) * P], table,
                                        start=True, stop=True)
                    ins.then_inc(er_done, 1)

                meta_rows(0)

                def group(g, q, last):
                    if not last:
                        meta_rows(g + 1)
                    turn(g, q, 0)
                    for b in range(GB):
                        if b + 1 < GB:
                            turn(g, q, b + 1)
                        right_logits(g, b)
                    pe.wait_ge(e_ready, g + 1)
                    pe.transpose(psS[:, S_ET:S_ET + P], e_sb[:, 1], ident).then_inc(eT_ready, 1)
                    pe.wait_ge(spread_ready, g + 1)
                    pe.matmul(psS[0:HEADS, S_LV:S_LV + 5 * GU], selh, spread[:].rearrange("p k u -> p (k u)"),
                              start=True, stop=True).then_inc(lv_ready, 1)
                    pe.wait_ge(yz_ready, g + 1)
                    pe.matmul(psS[:, S_PHI:S_PHI + HEADS], first_hot[:], phi_diag[:], start=True, stop=True)
                    pe.matmul(psS[:, S_YZ:S_YZ + 2 * GU], selht, yz[:].rearrange("p y u -> p (y u)"),
                              start=True, stop=True).then_inc(yzT_ready, 1)
                    pe.wait_ge(dn_ready, g + 1)
                    pe.transpose(psS[:, S_DT:S_DT + P], dn[:], ident).then_inc(dnT_ready, 1)
                    for b in range(GB):
                        pe.wait_ge(scaled, GB * g + b + 1)
                        pe.wait_ge(sum_used, GB * g + b + 1)
                        for k in range(BLK):
                            ins = pe.matmul(psP[:, b % 2, 0:FW], hot[:, q, b * BLK + k], gath[:, q, b * BLK + k],
                                            start=k == 0, stop=k == BLK - 1)
                        ins.then_inc(sum_ready, 1)

                each_group(pe, group)


def route_stage(nc, sb, bias, wr, br, slots_x):
    with ExitStack() as ctx:
        def t(name, shape, dt=F32):
            return ctx.enter_context(nc.sbuf_tensor(name, shape, dt))

        def sem(name):
            return ctx.enter_context(nc.semaphore(name))

        TE = TILES * EXPERTS
        cst, acc, xs, slot_i, weight = sb["cst"], sb["acc"], sb["xs"], sb["slot_i"], sb["weight"]
        ident = cst[:, C_ID:C_ID + P]
        bias_all = t("bias_all", [P, D])
        wr_sb = t("wr_sb", [P, KD, EXPERTS])
        br_all = t("br_all", [P, EXPERTS])
        rden = t("rden", [P, TILES, HEADS])
        stats = t("stats_r", [P, TILES, 6])
        mean = t("mean_r", [P, TILES])
        std = t("std_r", [P, TILES])
        rstd = t("rstd_r", [P, TILES])
        eps = t("eps_r", [P, 1])
        ones = t("ones_r", [P, P])
        xt = t("xt", [P, TILES, D])
        xtT = t("xtT", [P, 2, KD, P])
        prob = t("prob", [P, TILES, EXPERTS])
        left = t("left", [P, TILES, EXPERTS])
        work = t("work", [P, TILES, EXPERTS])
        hot1 = t("hot1", [P, TILES, EXPERTS])
        hot2 = t("hot2", [P, TILES, EXPERTS])
        top = t("top", [P, 2, TILES])
        col = t("col", [P, TILES])
        mask = t("mask", [P, EXPERTS, TILES])
        keep = t("keep", [P, EXPERTS, TILES])
        upto = t("upto", [P, EXPERTS, TILES])
        place = t("place", [P, EXPERTS, TILES])
        need_i = t("need_i", [P, EXPERTS], I32)
        need = t("need", [P, EXPERTS])
        ends = t("ends", [P, EXPERTS])
        base = t("base", [P, EXPERTS])
        slot_f = t("slot_f", [P, 2, TILES])
        done = t("done", [1, SLOT_TILES, EXPERTS])
        owner = t("owner", [1, SLOT_TILES])
        xn = t("xn", [P, 2, D])
        slot_col = t("slot_col", [P, 2, 2], I32)
        psT = ctx.enter_context(nc.psum_tensor("psT_r", [P, 2, 512], F32))
        psL = ctx.enter_context(nc.psum_tensor("psL", [P, 512], F32))
        psC = ctx.enter_context(nc.psum_tensor("psC_r", [P, 2, 512], F32))
        small_in = sem("small_in")
        v_step = sem("v_step_route")
        var_ready, std_ready = sem("var_ready_r"), sem("std_ready_r")
        xt_ready, xtT_ready, xtT_copied = sem("xt_ready"), sem("xtT_ready"), sem("xtT_copied")
        logits_ready, shifted, exped = sem("logits_ready"), sem("shifted"), sem("exped")
        mask_ready, counted = sem("mask_ready"), sem("counted_r")
        xn_ready = sem("xn_ready")
        carrier = sem("carrier_r")
        scattered = [sem("scattered0"), sem("scattered1")]

        def tile(ap, i):
            return ap[:, bass.ds(i, 1), :].rearrange("p a f -> p (a f)")

        with nc.Block() as block:
            @block.sync
            def _(sp):
                sp.dma_start(bias_all[:], bias.to_broadcast([P, D])).then_inc(small_in, 16)
                sp.dma_start(wr_sb[:], wr.rearrange("(k p) e -> p k e", p=P)).then_inc(small_in, 16)
                sp.dma_start(br_all[:], br.to_broadcast([P, EXPERTS])).then_inc(small_in, 16)

            @block.scalar
            def _(act):
                act.wait_ge(var_ready, 1)
                act.activation(std[:], std[:], ACT.Sqrt, bias=eps[:]).then_inc(std_ready, 1)
                with act.Fori(0, TILES // 2) as i:
                    for q in range(2):
                        act.wait_ge(xtT_ready, i * 2 + q + 1)
                        act.copy(xtT[:, q].rearrange("p k c -> p (k c)"), psT[:, q, 0:D]).then_inc(xtT_copied, 1)
                act.wait_ge(var_ready, 2)
                act.activation(std[:], std[:], ACT.Sqrt, bias=eps[:]).then_inc(std_ready, 1)
                act.wait_ge(shifted, 1)
                act.activation(prob[:], prob[:], ACT.Exp).then_inc(exped, 1)

            @block.tensor
            def _(pe):
                pe.wait_ge(small_in, 48)
                for i in range(TILES):
                    pe.wait_ge(xt_ready, i + 1)
                    if i >= 2:
                        pe.wait_ge(xtT_copied, i - 1)
                    for k in range(KD):
                        ins = pe.transpose(psT[:, i % 2, k * P:(k + 1) * P], xt[:, i, k * P:(k + 1) * P], ident)
                    ins.then_inc(xtT_ready, 1)
                    for j in ([i - 1] if i >= 1 else []) + ([i] if i == TILES - 1 else []):
                        pe.wait_ge(xtT_copied, j + 1)
                        for k in range(KD):
                            ins = pe.matmul(psL[:, j * EXPERTS:(j + 1) * EXPERTS], xtT[:, j % 2, k], wr_sb[:, k],
                                            start=k == 0, stop=k == KD - 1)
                ins.then_inc(logits_ready, 1)
                pe.wait_ge(mask_ready, 1)
                counts = mask[:].rearrange("p e t -> p (e t)")
                pe.matmul(psC[:, 0, 0:TE], cst[:, C_TRI:C_TRI + P], counts, start=True, stop=True)
                pe.matmul(psC[:, 1, 0:TE], ones[:], counts, start=True, stop=True).then_inc(counted, 1)

            @block.vector
            def _(dve):
                step = Chain(dve, v_step)

                def norms(of, n):
                    with dve.Fori(0, TILES) as i:
                        dve.bn_stats(tile(stats, i), tile(of, i)).then_inc(v_step, 1)
                    dve.wait_ge(v_step, step.n + TILES)
                    step.n += TILES
                    mean_var(dve, step, stats, mean[:], std[:])
                    dve.sem_inc(var_ready, 1)
                    dve.wait_ge(std_ready, n)
                    step(dve.reciprocal(rstd[:], std[:]))

                step(dve.memset(eps[:], EPS))
                dve.memset(ones[:], 1.0)
                step(dve.memset(keep[:], 1.0))
                step(dve.memset(keep[:, :, 0:1], 0.0))
                step(dve.tensor_scalar(rden[:], acc[:, :, D:FW], 1e-30, None, ALU.max))
                step(dve.reciprocal(rden[:], rden[:]))
                dve.wait_ge(small_in, 48)
                for h in range(HEADS):
                    part = acc[:, :, h * HD:(h + 1) * HD]
                    ins = dve.tensor_tensor(part, part, rden[:, :, h:h + 1].to_broadcast([P, TILES, HD]), ALU.mult)
                step(ins)
                step(dve.tensor_tensor(acc[:, :, 0:D], acc[:, :, 0:D], bias_all[:].unsqueeze(1).to_broadcast([P, TILES, D]), ALU.add))
                step(dve.tensor_tensor(xs[:], xs[:], acc[:, :, 0:D], ALU.add))
                norms(xs, 1)
                with dve.Fori(0, TILES) as i:
                    dve.tensor_scalar(tile(xt, i), tile(xs, i), mean[:, bass.ds(i, 1)], rstd[:, bass.ds(i, 1)],
                                      ALU.subtract, ALU.mult).then_inc(xt_ready, 1)
                dve.wait_ge(xt_ready, TILES)
                norms(xt, 2)
                per = [P, TILES, EXPERTS]
                dve.wait_ge(logits_ready, 1)
                step(dve.tensor_tensor(prob[:], psL[:, 0:TE].rearrange("p (t e) -> p t e", e=EXPERTS),
                                       br_all[:].unsqueeze(1).to_broadcast(per), ALU.add))
                step(dve.tensor_reduce(col[:], prob[:], AX.X, ALU.max))
                step(dve.tensor_tensor(prob[:], prob[:], col[:].unsqueeze(2).to_broadcast(per), ALU.subtract))
                dve.sem_inc(shifted, 1)
                dve.wait_ge(exped, 1)
                step(dve.tensor_reduce(col[:], prob[:], AX.X, ALU.add))
                step(dve.reciprocal(col[:], col[:]))
                step(dve.tensor_tensor(prob[:], prob[:], col[:].unsqueeze(2).to_broadcast(per), ALU.mult))
                iota = cst[:, C_IOTA8:C_IOTA8 + EXPERTS].unsqueeze(1).to_broadcast(per)
                for k, (of, hot) in enumerate(((prob, hot1), (left, hot2))):
                    step(dve.tensor_reduce(top[:, k], of[:], AX.X, ALU.max))
                    step(dve.tensor_tensor(work[:], of[:], top[:, k].unsqueeze(2).to_broadcast(per), ALU.not_equal))
                    step(dve.scalar_tensor_tensor(work[:], work[:], float(EXPERTS), iota, ALU.mult, ALU.add))
                    step(dve.tensor_reduce(col[:], work[:], AX.X, ALU.min))
                    step(dve.tensor_tensor(hot[:], iota, col[:].unsqueeze(2).to_broadcast(per), ALU.is_equal))
                    if k == 0:
                        step(dve.scalar_tensor_tensor(left[:], hot1[:], -2.0, prob[:], ALU.mult, ALU.add))
                step(dve.tensor_tensor(col[:], top[:, 0], top[:, 1], ALU.add))
                step(dve.reciprocal(col[:], col[:]))
                dve.tensor_tensor(weight[:], top[:], col[:].unsqueeze(1).to_broadcast([P, 2, TILES]), ALU.mult)
                step(dve.tensor_tensor(mask[:], hot1[:].rearrange("p t e -> p e t"), hot2[:].rearrange("p t e -> p e t"), ALU.add))
                dve.sem_inc(mask_ready, 1)
                dve.wait_ge(counted, 1)
                flat = "p e t -> p (e t)"
                step(dve.tensor_tensor_scan(upto[:].rearrange(flat), keep[:].rearrange(flat), psC[:, 1, 0:TE], 0.0, ALU.mult, ALU.add))
                step(dve.tensor_scalar(need[:], upto[:, :, TILES - 1], float(SLOT_TILE - 1), None, ALU.add))
                step(dve.tensor_copy(need_i[:], need[:]))
                step(dve.tensor_scalar(need_i[:], need_i[:], SLOT_TILE.bit_length() - 1, None, ALU.arith_shift_right))
                step(dve.tensor_copy(need[:], need_i[:]))
                step(dve.tensor_scalar(need[:], need[:], float(SLOT_TILE), None, ALU.mult))
                step(dve.tensor_tensor_scan(ends[:], ones[:, 0:EXPERTS], need[:], 0.0, ALU.mult, ALU.add))
                step(dve.tensor_tensor(base[:], ends[:], need[:], ALU.subtract))
                step(dve.tensor_tensor(place[:].rearrange(flat), upto[:].rearrange(flat), psC[:, 1, 0:TE], ALU.subtract))
                step(dve.tensor_tensor(place[:].rearrange(flat), place[:].rearrange(flat), psC[:, 0, 0:TE], ALU.add))
                step(dve.tensor_tensor(place[:], place[:], base[:].unsqueeze(2).to_broadcast([P, EXPERTS, TILES]), ALU.add))
                for k, hot in enumerate((hot1, hot2)):
                    step(dve.tensor_tensor(work[:], hot[:], place[:].rearrange("p e t -> p t e"), ALU.mult))
                    step(dve.tensor_reduce(slot_f[:, k], work[:], AX.X, ALU.add))
                step(dve.tensor_copy(slot_i[:], slot_f[:]))
                step(dve.tensor_tensor(done[:], ends[0:1].unsqueeze(1).to_broadcast([1, SLOT_TILES, EXPERTS]),
                                       cst[0:1, C_SLOT:C_SLOT + SLOT_TILES].unsqueeze(2).to_broadcast([1, SLOT_TILES, EXPERTS]), ALU.is_le))
                step(dve.tensor_reduce(owner[:], done[:], AX.X, ALU.add))
                step(dve.tensor_scalar(owner[:], owner[:], float(EXPERTS - 1), None, ALU.min))
                step(dve.tensor_copy(sb["expert_of"][:], owner[:]))
                def to_send(at, q):
                    dve.tensor_copy(slot_col[:, q], slot_i[:, :, bass.ds(at, 1)].rearrange("p k a -> p (k a)"))
                    dve.tensor_scalar(xn[:, q], tile(xt, at), mean[:, bass.ds(at, 1)], rstd[:, bass.ds(at, 1)],
                                      ALU.subtract, ALU.mult).then_inc(xn_ready, 1)

                to_send(0, 0)
                to_send(1, 1)
                with dve.Fori(1, TILES // 2) as i:
                    for q in range(2):
                        dve.wait_ge(scattered[q], i * 32)
                        to_send(i * 2 + q, q)

            @block.gpsimd
            def _(pool):
                with pool.Fori(0, TILES // 2) as i:
                    for q in range(2):
                        wait_apart(pool, xn_ready, i * 2 + q + 1, carrier)
                        for k in range(2):
                            pool.indirect_dma_start(slots_x, bass.IndirectOffsetOnAxis(ap=slot_col[:, q, k:k + 1], axis=0),
                                                    xn[:, q], None).then_inc(scattered[q], 16)
                for q in range(2):
                    pool.wait_ge(scattered[q], 32 * (TILES // 2))


def expert_stage(nc, sb, experts, b2, slots_x, slots_y):
    with ExitStack() as ctx:
        def t(name, shape, dt=F32):
            return ctx.enter_context(nc.sbuf_tensor(name, shape, dt))

        def sem(name):
            return ctx.enter_context(nc.semaphore(name))

        HALVES = SLOT_TILE // P
        ident = sb["cst"][:, C_ID:C_ID + P]
        wbuf = t("wbuf", [P, 2, E_W])
        b2_all = t("b2_all", [P, 2, D])
        xrow = t("xrow", [P, 2, HALVES, D])
        xeT = t("xeT", [P, 2, KD, SLOT_TILE])
        hT = t("hT", [P, KH, SLOT_TILE])
        yrow = t("yrow", [P, 2, HALVES, D])
        psX = ctx.enter_context(nc.psum_tensor("psX", [P, 2, 512], F32))
        psH = ctx.enter_context(nc.psum_tensor("psH", [P, 2, 512], F32))
        psY = ctx.enter_context(nc.psum_tensor("psY", [P, HALVES, 512], F32))
        w_in = [sem("w_in0"), sem("w_in1")]
        x_in = [sem("x_in0"), sem("x_in1")]
        y_stored = [sem("y_stored0"), sem("y_stored1")]
        xT_ready, xe_ready = sem("xT_ready_e"), sem("xe_ready")
        h_ready, h_used, gelu_done = sem("h_ready"), sem("h_used"), sem("gelu_done")
        y_ready, y_copied = sem("y_ready"), sem("y_copied")
        tile_done = sem("tile_done")

        def w1(q, k, m):
            return wbuf[:, q, k * HID + m * P:k * HID + (m + 1) * P]

        def w2(q, m):
            return wbuf[:, q, E_W2 + m * D:E_W2 + (m + 1) * D]

        def each_tile(eng, body, last_too=True):
            with eng.Fori(0, (SLOT_TILES - 1) // 2) as i:
                body(i * 2, 0, False)
                body(i * 2 + 1, 1, False)
            body(SLOT_TILES - 1, 0, True)
        assert SLOT_TILES % 2 == 1

        with nc.Block() as block:
            @block.sync
            def _(sp):
                def load(s, q):
                    e = sp.value_load(sb["expert_of"][0:1, bass.ds(s, 1)], min_val=0, max_val=EXPERTS - 1)
                    sp.dma_start(wbuf[:, q], experts[bass.ds(e * P, P), :]).then_inc(w_in[q], 16)
                    sp.dma_start(b2_all[:, q], b2[bass.ds(e, 1), :].to_broadcast([P, D])).then_inc(w_in[q], 16)
                    sp.dma_start(xrow[:, q], slots_x[bass.ds(s * SLOT_TILE, SLOT_TILE), :].rearrange(
                        "(j p) f -> p j f", p=P)).then_inc(x_in[q], 16)

                load(0, 0)
                sp.sem_inc(tile_done, 1)

                def body(s, q, last):
                    if not last:
                        sp.wait_ge(tile_done, s + 1)
                        load(s + 1, 1 - q)
                    sp.wait_ge(y_copied, s * HALVES + 2 * HALVES)
                    sp.dma_start(slots_y[bass.ds(s * SLOT_TILE, SLOT_TILE), :].rearrange("(j p) f -> p j f", p=P),
                                 yrow[:, q]).then_inc(y_stored[q], 16)

                each_tile(sp, body)
                sp.wait_ge(y_stored[0], 16 + 16 * (SLOT_TILES // 2 + 1))
                sp.wait_ge(y_stored[1], 16 + 16 * (SLOT_TILES // 2))

            @block.tensor
            def _(pe):
                def turn(s, q):
                    pe.wait_ge(x_in[q], (s - q) * 8 + 16)
                    for k in range(KD):
                        for j in range(HALVES):
                            ins = pe.transpose(psX[:, q, k * SLOT_TILE + j * P:k * SLOT_TILE + (j + 1) * P],
                                               xrow[:, q, j, k * P:(k + 1) * P], ident)
                    ins.then_inc(xT_ready, 1)

                turn(0, 0)

                def body(s, q, last):
                    pe.wait_ge(xe_ready, s + 1)
                    for m in range(KH):
                        if m % 2 == 0:
                            pe.wait_ge(h_used, s * KH + m + 2)
                        for k in range(KD):
                            ins = pe.matmul(psH[:, m // 2 % 2, (m % 2) * SLOT_TILE:(m % 2 + 1) * SLOT_TILE], w1(q, k, m),
                                            xeT[:, q, k], start=k == 0, stop=k == KD - 1)
                        if m % 2:
                            ins.then_inc(h_ready, 1)
                    if not last:
                        turn(s + 1, 1 - q)
                    pe.wait_ge(gelu_done, s + 1)
                    for j in range(HALVES):
                        pe.wait_ge(y_copied, s * HALVES + j + 1)
                        for m in range(KH):
                            ins = pe.matmul(psY[:, j, 0:D], hT[:, m, j * P:(j + 1) * P], w2(q, m),
                                            start=m == 0, stop=m == KH - 1)
                        ins.then_inc(y_ready, 1)

                each_tile(pe, body)

            @block.scalar
            def _(act):
                act.sem_inc(h_used, 4)

                def body(s, q, last):
                    act.wait_ge(xT_ready, s + 1)
                    act.wait_ge(w_in[q], (s - q) * 16 + 32)
                    for k in range(KD):
                        ins = act.activation(xeT[:, q, k], psX[:, q, k * SLOT_TILE:(k + 1) * SLOT_TILE], ACT.Identity,
                                             bias=wbuf[:, q, E_B + k:E_B + k + 1], scale=wbuf[:, q, E_G + k:E_G + k + 1])
                    ins.then_inc(xe_ready, 1)
                    act.wait_ge(y_copied, s * HALVES + HALVES)
                    for m in range(KH):
                        act.wait_ge(h_ready, s * (KH // 2) + m // 2 + 1)
                        act.activation(hT[:, m], psH[:, m // 2 % 2, (m % 2) * SLOT_TILE:(m % 2 + 1) * SLOT_TILE], ACT.Gelu,
                                       bias=wbuf[:, q, E_B1 + m:E_B1 + m + 1]).then_inc(h_used, 1)
                    act.wait_ge(h_used, s * KH + KH + 4)
                    act.sem_inc(gelu_done, 1)

                each_tile(act, body)

            @block.vector
            def _(dve):
                dve.sem_inc(y_copied, HALVES)
                dve.sem_inc(y_stored[0], 16)
                dve.sem_inc(y_stored[1], 16)

                def body(s, q, last):
                    dve.wait_ge(y_stored[q], (s - q) * 8 + 16)
                    for j in range(HALVES):
                        dve.wait_ge(y_ready, s * HALVES + j + 1)
                        dve.tensor_tensor(yrow[:, q, j], psY[:, j, 0:D], b2_all[:, q], ALU.add).then_inc(y_copied, 1)
                    dve.wait_ge(y_copied, s * HALVES + 2 * HALVES)
                    dve.sem_inc(tile_done, 1)

                each_tile(dve, body)


def combine_stage(nc, sb, slots_y, out):
    with ExitStack() as ctx:
        xs, weight = sb["xs"], sb["weight"]
        slot_col = ctx.enter_context(nc.sbuf_tensor("slot_col_c", [P, 4, 2], I32))
        ys = ctx.enter_context(nc.sbuf_tensor("ys", [P, 4, 2, D], F32))
        copied = ctx.enter_context(nc.semaphore("slots_copied"))
        landed = [ctx.enter_context(nc.semaphore(f"y_landed{q}")) for q in range(4)]
        carrier = ctx.enter_context(nc.semaphore("carrier_c"))
        half = ctx.enter_context(nc.semaphore("half_summed"))
        summed = ctx.enter_context(nc.semaphore("summed"))
        stored = ctx.enter_context(nc.semaphore("out_stored"))
        WHOLE = TILES // 2

        with nc.Block() as block:
            @block.gpsimd
            def _(pool):
                with pool.Fori(0, WHOLE) as i:
                    for q in range(2):
                        at = i * 2 + q
                        pool.wait_ge(summed, at + 1)
                        pool.tensor_copy(slot_col[:, q], sb["slot_i"][:, :, bass.ds(at, 1)].rearrange(
                            "p k a -> p (k a)")).then_inc(copied, 1)
                        wait_apart(pool, copied, at + 1, carrier)
                        for k in range(2):
                            pool.indirect_dma_start(ys[:, q, k], None, slots_y, bass.IndirectOffsetOnAxis(
                                ap=slot_col[:, q, k:k + 1], axis=0)).then_inc(landed[q], 16)

            @block.vector
            def _(dve):
                dve.sem_inc(summed, 2)
                with dve.Fori(0, WHOLE) as i:
                    for q in range(2):
                        at = i * 2 + q
                        row = xs[:, bass.ds(at, 1), :].rearrange("p a f -> p (a f)")
                        dve.wait_ge(landed[q], i * 32 + 32)
                        dve.scalar_tensor_tensor(row, ys[:, q, 0], weight[:, 0, bass.ds(at, 1)], row,
                                                 ALU.mult, ALU.add).then_inc(half, 1)
                        dve.wait_ge(half, at + 1)
                        dve.scalar_tensor_tensor(row, ys[:, q, 1], weight[:, 1, bass.ds(at, 1)], row,
                                                 ALU.mult, ALU.add).then_inc(summed, 1)

            @block.sync
            def _(sp):
                with sp.Fori(0, TILES) as i:
                    sp.wait_ge(summed, i + 3)
                    sp.dma_start(out[bass.ds(i * P, P), :], xs[:, bass.ds(i, 1), :].rearrange("p a f -> p (a f)")).then_inc(stored, 16)
                sp.wait_ge(stored, 16 * TILES)


def build(nc, ins, out):
    feats = nc.dram_tensor("feats", (ROWS * RELS, FW), F32, kind="Internal").ap()
    slots_x = nc.dram_tensor("slots_x", (SLOTS, D), F32, kind="Internal").ap()
    slots_y = nc.dram_tensor("slots_y", (SLOTS, D), F32, kind="Internal").ap()
    with ExitStack() as ctx:
        def keep(name, shape, dt=F32):
            return ctx.enter_context(nc.sbuf_tensor(name, shape, dt))

        sb = {
            "cst": keep("cst", [P, C_W]),
            "xs": keep("xs", [P, TILES, D]),
            "er": keep("er", [P, TILES, RELS * HEADS]),
            "acc": keep("acc", [P, TILES, FW]),
            "tile_of": keep("tile_of", [P, GROUPS]),
            "row_of": keep("row_of", [P, GROUPS], I32),
            "pair_tile": keep("pair_tile", [1, GROUPS, GB], I32),
            "slot_i": keep("slot_i", [P, 2, TILES], I32),
            "weight": keep("weight", [P, 2, TILES]),
            "expert_of": keep("expert_of", [1, SLOT_TILES], I32),
        }
        node_stage(nc, sb, ins["x"], ins["conv"], ins["attn_l"], ins["attn_r"], feats, slots_x, ins["consts"])
        schedule_stage(nc, sb, ins["edges"])
        edge_stage(nc, sb, ins["edges"], feats)
        route_stage(nc, sb, ins["bias"], ins["wr"], ins["br"], slots_x)
        expert_stage(nc, sb, ins["experts"], ins["b2"], slots_x, slots_y)
        combine_stage(nc, sb, slots_y, out)


def kernel(x, src, dst, edge_type_8, L0_gnn_conv_weights, L0_gnn_attn_l, L0_gnn_attn_r, L0_gnn_h_bias, L0_ffn_Wr,
           L0_ffn_br, L0_ffn_ln_g, L0_ffn_ln_b, L0_ffn_W1, L0_ffn_b1, L0_ffn_W2, L0_ffn_b2):
    import concourse.bacc as bacc
    from concourse.bass_utils import run_bass_kernel_spmd

    def padded(a, rows, fill=0):
        a = np.asarray(a)
        return np.concatenate([a, np.full((rows - a.shape[0],) + a.shape[1:], fill, a.dtype)])

    def chunks(a, fill):
        return padded(a, CHUNK_ROWS * UNIT, fill).reshape(CHUNK_ROWS, UNIT)

    def columns(a, chunk):
        return np.asarray(a).reshape(EXPERTS, chunk, P).transpose(0, 2, 1)

    w1 = np.asarray(L0_ffn_W1).reshape(EXPERTS, KD, P, HID).transpose(0, 2, 1, 3).reshape(EXPERTS, P, KD * HID)
    w2 = np.asarray(L0_ffn_W2).reshape(EXPERTS, KH, P, D).transpose(0, 2, 1, 3).reshape(EXPERTS, P, KH * D)
    experts = np.concatenate([w1, w2, columns(L0_ffn_ln_g, KD), columns(L0_ffn_ln_b, KD), columns(L0_ffn_b1, KH)], 2)
    arrays = {
        "x": padded(x, ROWS),
        "edges": np.stack([chunks(dst, ROWS), chunks(src, 0), chunks(edge_type_8, 0)], 1),
        "conv": np.asarray(L0_gnn_conv_weights).transpose(2, 0, 1, 3).reshape(D, RELS * D),
        "attn_l": np.asarray(L0_gnn_attn_l).reshape(1, RELS * D),
        "attn_r": np.asarray(L0_gnn_attn_r).reshape(1, RELS * D),
        "bias": np.asarray(L0_gnn_h_bias).reshape(1, D),
        "wr": np.asarray(L0_ffn_Wr),
        "br": np.asarray(L0_ffn_br).reshape(1, EXPERTS),
        "experts": experts.reshape(EXPERTS * P, E_W),
        "b2": np.asarray(L0_ffn_b2),
        "consts": constants(),
    }
    arrays = {name: np.ascontiguousarray(a) for name, a in arrays.items()}
    nc = bacc.Bacc("TRN2", target_bir_lowering=False, num_devices=1)
    ins = {name: nc.dram_tensor(f"in_{name}", a.shape, mybir.dt.from_np(a.dtype), kind="ExternalInput").ap()
           for name, a in arrays.items()}
    out = nc.dram_tensor("out", (ROWS, D), F32, kind="ExternalOutput").ap()
    build(nc, ins, out)
    r = run_bass_kernel_spmd(nc, [{f"in_{name}": a for name, a in arrays.items()}], core_ids=[0])
    return r.results[0]["out"][:N_NODES]
```

```python
from contextlib import ExitStack

import numpy as np
import concourse.bass as bass
import concourse.mybir as mybir

F32 = mybir.dt.float32
I32 = mybir.dt.int32
U32 = mybir.dt.uint32
ALU = mybir.AluOpType
ACT = mybir.ActivationFunctionType
AX = mybir.AxisListType

P = 128
N_NODES = 3750
N_EDGES = 120000
D = 256
HEADS = 4
HD = D // HEADS
RELS = 8
EXPERTS = 8
HID = 1024
TILES = -(-N_NODES // P)
ROWS = TILES * P
KD = D // P
KH = HID // P

FW = D + HEADS
UNIT = 128
BLK = 4
EBLOCKS = -(-N_EDGES // (BLK * UNIT))
CHUNK_ROWS = EBLOCKS * BLK
PAIRS = EBLOCKS + TILES - 1
GB = 8
GROUPS = PAIRS // GB
GU = GB * BLK
assert GROUPS * GB == PAIRS and GU * HEADS == P
BIG = 1.0e38
EPS = 1e-5
SLOPE = 0.2
LBP = 47
LBJ = EBLOCKS // LBP
assert LBP * LBJ == EBLOCKS

SLOT_TILE = 256
SLOT_TILES = (2 * ROWS + EXPERTS * (SLOT_TILE - 1)) // SLOT_TILE
SLOTS = SLOT_TILES * SLOT_TILE

E_W2 = KD * HID
E_G = E_W2 + KH * D
E_B = E_G + KD
E_B1 = E_B + KD
E_W = E_B1 + KH

C_ID, C_IOTA, C_MASKU, C_SELH, C_IOTA8, C_PAIR, C_CHUNK, C_THR, C_TILE, C_SELHT, C_TRI, C_SLOT = (
    0, 128, 256, 288, 292, 300, 333, 334, 363, 392, 520, 648)
C_W = C_SLOT + SLOT_TILES


def constants():
    c = np.zeros((P, C_W), np.float32)
    p = np.arange(P)
    c[:, C_ID:C_ID + P] = np.eye(P)
    c[:, C_IOTA:C_IOTA + P] = p[None, :]
    c[:, C_MASKU:C_MASKU + GU] = p[:, None] // HEADS == np.arange(GU)[None, :]
    c[:, C_SELH:C_SELH + HEADS] = p[:, None] % HEADS == np.arange(HEADS)[None, :]
    c[:, C_IOTA8:C_IOTA8 + RELS] = np.arange(RELS)[None, :]
    c[:, C_PAIR:C_PAIR + GROUPS] = GB * np.arange(GROUPS)[None, :] + p[:, None] // (HEADS * BLK)
    c[:, C_CHUNK] = p // HEADS % BLK
    c[:, C_THR:C_THR + TILES - 1] = P * (np.arange(TILES - 1)[None, :] + 1)
    c[:, C_TILE:C_TILE + TILES - 1] = np.arange(TILES - 1)[None, :]
    c[:HEADS, C_SELHT:C_SELHT + P] = p[None, :] % HEADS == np.arange(HEADS)[:, None]
    c[:, C_TRI:C_TRI + P] = p[:, None] < p[None, :]
    c[:, C_SLOT:C_SLOT + SLOT_TILES] = SLOT_TILE * np.arange(SLOT_TILES)[None, :]
    return c


class Chain:

    def __init__(self, eng, sem):
        self.eng, self.sem, self.base, self.n = eng, sem, 0, 0

    def start(self, base):
        self.base, self.n = base, 0

    def __call__(self, ins):
        ins.then_inc(self.sem, 1)
        self.n += 1
        self.eng.wait_ge(self.sem, self.base + self.n)


def wait_apart(pool, sem, value, carrier):
    pool.wait_ge(sem, value)
    pool.sem_inc(carrier, 1)


def mean_var(dve, step, stats, mean, var):
    even, odd = stats[:, :, 1], stats[:, :, 4]
    dve.tensor_tensor(mean, even, odd, ALU.subtract)
    step(dve.tensor_tensor(var, stats[:, :, 2], stats[:, :, 5], ALU.add))
    step(dve.scalar_tensor_tensor(mean, mean, 0.25, mean, ALU.mult, ALU.mult))
    step(dve.scalar_tensor_tensor(var, var, 1.0 / D, mean, ALU.mult, ALU.add))
    step(dve.tensor_tensor(mean, even, odd, ALU.add))
    step(dve.tensor_scalar(mean, mean, 0.5, None, ALU.mult))


def node_stage(nc, sb, x, conv, attn_l, attn_r, feats, slots_x, cst_dram):
    with ExitStack() as ctx:
        def t(name, shape, dt=F32):
            return ctx.enter_context(nc.sbuf_tensor(name, shape, dt))

        def sem(name):
            return ctx.enter_context(nc.semaphore(name))

        wext = t("wext", [P, KD, RELS, FW])
        wer = t("wer", [P, KD, RELS, HEADS])
        attn = t("attn", [P, 2, RELS * D])
        prod = t("prod", [P, RELS * D])
        stats = t("stats", [P, TILES, 6])
        mean = t("mean", [P, TILES])
        std = t("std", [P, TILES])
        rstd = t("rstd", [P, TILES])
        eps = t("eps", [P, 1])
        xh = t("xh", [P, 2, D])
        xT = t("xT", [P, 2, KD, P])
        frow = t("frow", [P, 2, RELS, FW])
        psF = ctx.enter_context(nc.psum_tensor("psF", [P, 2, 2, 512], F32))
        psT = ctx.enter_context(nc.psum_tensor("psT", [P, 2, 512], F32))
        psR = ctx.enter_context(nc.psum_tensor("psR", [P, 2, 512], F32))
        cst_in, x_in, w_in, a_in = sem("cst_in"), sem("x_in"), sem("w_in"), sem("a_in")
        v_step = sem("v_step")
        var_ready, std_ready = sem("var_ready"), sem("std_ready")
        w_ready = sem("w_ready")
        acc_zero, slots_zero = sem("acc_zero"), sem("slots_zero")
        xh_ready, xT_ready, xT_copied = sem("xh_ready"), sem("xT_ready"), sem("xT_copied")
        er_ready, er_copied = sem("er_ready"), sem("er_copied")
        pair_ready = [sem("pair_ready_act"), sem("pair_ready_dve")]
        pair_copied = [sem("pair_copied_act"), sem("pair_copied_dve")]
        row_stored = [sem("row_stored0"), sem("row_stored1")]
        xs, er_sb, cst, acc = sb["xs"], sb["er"], sb["cst"], sb["acc"]
        ident = cst[:, C_ID:C_ID + P]
        feats_tiles = feats.rearrange("(n r) w -> n (r w)", r=RELS)

        with nc.Block() as block:
            @block.sync
            def _(sp):
                sp.dma_start(cst[:], cst_dram).then_inc(cst_in, 16)
                sp.dma_start(xs[:], x.rearrange("(t p) f -> p t f", p=P)).then_inc(x_in, 16)
                for k in range(KD):
                    for r in range(RELS):
                        sp.dma_start(wext[:, k, r, 0:D], conv[k * P:(k + 1) * P, r * D:(r + 1) * D]).then_inc(w_in, 16)
                for a, src in enumerate((attn_l, attn_r)):
                    sp.dma_start(attn[:, a, :], src.to_broadcast([P, RELS * D])).then_inc(a_in, 16)
                sp.wait_ge(acc_zero, 1)
                for k in range(SLOTS // P):
                    sp.dma_start(slots_x[k * P:(k + 1) * P, :], acc[:, 0, 0:D]).then_inc(slots_zero, 16)
                sp.sem_inc(row_stored[0], 16)
                sp.sem_inc(row_stored[1], 16)
                with sp.Fori(0, TILES // 2) as i:
                    for q in range(2):
                        sp.wait_ge(pair_copied[0], i * 4 + 2 * q + 3)
                        sp.wait_ge(pair_copied[1], i * 4 + 2 * q + 3)
                        sp.dma_start(feats_tiles[bass.ds(i * 256 + q * P, P), :],
                                     frow[:, q].rearrange("p r w -> p (r w)")).then_inc(row_stored[q], 16)
                for q in range(2):
                    sp.wait_ge(row_stored[q], 16 * (TILES // 2 + 1))
                sp.wait_ge(slots_zero, 16 * (SLOTS // P))

            @block.vector
            def _(dve):
                step = Chain(dve, v_step)
                dve.sem_inc(pair_copied[1], 1)
                dve.sem_inc(er_copied, 2)
                dve.memset(acc[:], 0.0).then_inc(acc_zero, 1)
                step(dve.memset(eps[:], EPS))
                dve.wait_ge(x_in, 16)
                with dve.Fori(0, TILES) as i:
                    dve.bn_stats(stats[:, bass.ds(i, 1), :].rearrange("p a c -> p (a c)"),
                                 xs[:, bass.ds(i, 1), :].rearrange("p a f -> p (a f)")).then_inc(v_step, 1)
                dve.wait_ge(v_step, step.n + TILES)
                step.start(step.n + TILES)
                mean_var(dve, step, stats, mean[:], std[:])
                dve.sem_inc(var_ready, 1)
                dve.wait_ge(std_ready, 1)
                step(dve.reciprocal(rstd[:], std[:]))

                def normalise(t_, q):
                    at = bass.ds(t_, 1)
                    dve.tensor_scalar(xh[:, q], xs[:, at, :].rearrange("p a f -> p (a f)"), mean[:, at], rstd[:, at],
                                      ALU.subtract, ALU.mult).then_inc(xh_ready, 1)

                normalise(0, 0)
                normalise(1, 1)
                dve.wait_ge(w_in, 16 * KD * RELS)
                dve.wait_ge(a_in, 32)
                for k in range(KD):
                    for a in range(2):
                        step(dve.tensor_tensor(prod[:].rearrange("p (r c) -> p r c", r=RELS), wext[:, k, :, 0:D],
                                               attn[:, a, :].rearrange("p (r c) -> p r c", r=RELS), ALU.mult))
                        dst = wext[:, k, :, D:FW] if a == 0 else wer[:, k]
                        step(dve.tensor_reduce(dst, prod[:].rearrange("p (r h d) -> p r h d", r=RELS, h=HEADS),
                                               AX.X, ALU.add))
                dve.sem_inc(w_ready, 1)

                def finish(i, q, ahead):
                    dve.wait_ge(er_ready, i * 2 + q + 1)
                    dve.tensor_copy(er_sb[:, bass.ds(i * 2 + q, 1), :].rearrange("p a c -> p (a c)"),
                                    psR[:, q, 0:RELS * HEADS]).then_inc(er_copied, 1)
                    dve.wait_ge(row_stored[q], i * 16 + 16)
                    for pair in (1, 3):
                        dve.wait_ge(pair_ready[1], i * 4 + 2 * q + pair // 2 + 1)
                        dve.tensor_copy(frow[:, q, 2 * pair:2 * pair + 2], psF[:, 1, :, 0:FW]).then_inc(pair_copied[1], 1)
                    if ahead:
                        dve.wait_ge(xT_ready, i * 2 + q + 1)
                        normalise(i * 2 + q + 2, q)

                with dve.Fori(0, TILES // 2 - 1) as i:
                    finish(i, 0, True)
                    finish(i, 1, True)
                for q in range(2):
                    finish(TILES // 2 - 1, q, False)

            @block.scalar
            def _(act):
                act.sem_inc(pair_copied[0], 1)
                act.wait_ge(var_ready, 1)
                act.activation(std[:], std[:], ACT.Sqrt, bias=eps[:]).then_inc(std_ready, 1)
                with act.Fori(0, TILES // 2) as i:
                    for q in range(2):
                        act.wait_ge(xT_ready, i * 2 + q + 1)
                        act.copy(xT[:, q].rearrange("p k c -> p (k c)"), psT[:, q, 0:D]).then_inc(xT_copied, 1)
                        act.wait_ge(row_stored[q], i * 16 + 16)
                        for pair in (0, 2):
                            act.wait_ge(pair_ready[0], i * 4 + 2 * q + pair // 2 + 1)
                            act.copy(frow[:, q, 2 * pair:2 * pair + 2], psF[:, 0, :, 0:FW]).then_inc(pair_copied[0], 1)

            @block.tensor
            def _(pe):
                pe.wait_ge(cst_in, 16)

                def turn(i, q):
                    pe.wait_ge(xh_ready, i * 2 + q + 1)
                    for k in range(KD):
                        ins = pe.transpose(psT[:, q, k * P:(k + 1) * P], xh[:, q, k * P:(k + 1) * P], ident)
                    ins.then_inc(xT_ready, 1)

                def multiply(i, q):
                    pe.wait_ge(xT_copied, i * 2 + q + 1)
                    pe.wait_ge(er_copied, i * 2 + q + 1)
                    for k in range(KD):
                        ins = pe.matmul(psR[:, q, 0:RELS * HEADS], xT[:, q, k], wer[:, k].rearrange("p r h -> p (r h)"),
                                        start=k == 0, stop=k == KD - 1)
                    ins.then_inc(er_ready, 1)
                    for pair in range(4):
                        pe.wait_ge(pair_copied[pair % 2], i * 4 + 2 * q + pair // 2 + 1)
                        for j in range(2):
                            for k in range(KD):
                                ins = pe.matmul(psF[:, pair % 2, j, 0:FW], xT[:, q, k], wext[:, k, 2 * pair + j],
                                                start=k == 0, stop=k == KD - 1)
                        ins.then_inc(pair_ready[pair % 2], 1)

                turn(0, 0)
                pe.wait_ge(w_ready, 1)
                with pe.Fori(0, TILES // 2 - 1) as i:
                    turn(i, 1)
                    multiply(i, 0)
                    turn(i + 1, 0)
                    multiply(i, 1)
                turn(TILES // 2 - 1, 1)
                multiply(TILES // 2 - 1, 0)
                multiply(TILES // 2 - 1, 1)


def schedule_stage(nc, sb, edges):
    with ExitStack() as ctx:
        def t(name, shape, dt=F32):
            return ctx.enter_context(nc.sbuf_tensor(name, shape, dt))

        cst = sb["cst"]
        last_i = t("last_i", [LBP, LBJ, 1], I32)
        last_f = t("last_f", [LBP, LBJ])
        below = t("below", [LBP, LBJ, TILES - 1])
        belows = t("belows", [LBP, TILES - 1])
        ones = t("ones", [LBP, P])
        stairs = t("stairs", [P, TILES - 1])
        passed = t("passed", [P, GROUPS, TILES - 1])
        row = t("row", [P, GROUPS])
        reg_passed = t("reg_passed", [1, GROUPS, TILES - 1])
        pair_row = t("pair_row", [1, GROUPS, 1])
        reg_d = t("reg_d", [1, GROUPS])
        ps = ctx.enter_context(nc.psum_tensor("psC", [P, 512], F32))
        last_in = ctx.enter_context(nc.semaphore("last_in"))
        v_step = ctx.enter_context(nc.semaphore("v_step_schedule"))
        counted = ctx.enter_context(nc.semaphore("counted"))
        steps = TILES - 1
        last_of = edges.rearrange("(p j k) c e -> p j k c e", j=LBJ, k=BLK)[:, :, BLK - 1, 0, UNIT - 1:UNIT]

        with nc.Block() as block:
            @block.sync
            def _(sp):
                with nc.allow_non_contiguous_dma("one word of each edge block"):
                    sp.dma_start(last_i[:], last_of).then_inc(last_in, 16)

            @block.tensor
            def _(pe):
                pe.wait_ge(v_step, 4)
                pe.matmul(ps[:, 0:steps], ones[:], belows[:], start=True, stop=True).then_inc(counted, 1)

            @block.vector
            def _(dve):
                step = Chain(dve, v_step)
                step(dve.memset(ones[:], 1.0))
                dve.wait_ge(last_in, 16)
                step(dve.tensor_copy(last_f[:], last_i[:].rearrange("p j o -> p (j o)")))
                step(dve.tensor_tensor(below[:], last_f[:].unsqueeze(2).to_broadcast([LBP, LBJ, steps]),
                                       cst[0:LBP, C_THR:C_THR + steps].unsqueeze(1).to_broadcast([LBP, LBJ, steps]),
                                       ALU.is_lt))
                step(dve.tensor_reduce(belows[:], below[:].rearrange("p j d -> p d j"), AX.X, ALU.add))
                dve.wait_ge(counted, 1)
                step(dve.tensor_tensor(stairs[:], ps[:, 0:steps], cst[:, C_TILE:C_TILE + steps], ALU.add))
                pair = cst[:, C_PAIR:C_PAIR + GROUPS]
                step(dve.tensor_tensor(passed[:], stairs[:].unsqueeze(1).to_broadcast([P, GROUPS, steps]),
                                       pair.unsqueeze(2).to_broadcast([P, GROUPS, steps]), ALU.is_lt))
                step(dve.tensor_reduce(sb["tile_of"][:], passed[:], AX.X, ALU.add))
                step(dve.tensor_tensor(row[:], pair, sb["tile_of"][:], ALU.subtract))
                step(dve.tensor_scalar(row[:], row[:], float(BLK), cst[:, C_CHUNK:C_CHUNK + 1], ALU.mult, ALU.add))
                step(dve.tensor_copy(sb["row_of"][:], row[:]))
                for b in range(GB):
                    step(dve.tensor_scalar(reg_d[:], pair[0:1, :], float(b), None, ALU.add))
                    step(dve.tensor_tensor(reg_passed[:], stairs[0:1, :].unsqueeze(1).to_broadcast([1, GROUPS, steps]),
                                           reg_d[:].unsqueeze(2).to_broadcast([1, GROUPS, steps]), ALU.is_lt))
                    step(dve.tensor_reduce(pair_row[:].rearrange("p g o -> p (g o)"), reg_passed[:], AX.X, ALU.add))
                    step(dve.tensor_copy(sb["pair_tile"][:, :, b], pair_row[:].rearrange("p g o -> p (g o)")))


def edge_stage(nc, sb, edges, feats):
    with ExitStack() as ctx:
        def t(name, shape, dt=F32):
            return ctx.enter_context(nc.sbuf_tensor(name, shape, dt))

        def psum(name, shape):
            return ctx.enter_context(nc.psum_tensor(name, shape, F32))

        def sem(name):
            return ctx.enter_context(nc.semaphore(name))

        cst, acc, er_sb, pair_tile = sb["cst"], sb["acc"], sb["er"], sb["pair_tile"]
        ident = cst[:, C_ID:C_ID + P]
        iota = cst[:, C_IOTA:C_IOTA + P]
        masku = cst[:, C_MASKU:C_MASKU + GU]
        selh = cst[:, C_SELH:C_SELH + HEADS]
        selht = cst[0:HEADS, C_SELHT:C_SELHT + P]
        iota8 = cst[:, C_IOTA8:C_IOTA8 + RELS]
        row_col = t("row_col", [P, 2], I32)
        meta = t("meta", [P, 2, 3 * UNIT], I32)
        tile_col = t("tile_col", [P, 2])
        rows = t("rows", [P, 3, UNIT])
        reset = t("reset", [P, 2, UNIT + 1])
        cat = t("cat", [P, 2, 5])
        idxT = t("idxT", [P, 2, GU], I32)
        ndlT = t("ndlT", [P, 2, GU])
        square = t("square", [P, 2, BLK, P])
        typeT = t("typeT", [P, 2, GU, RELS])
        gath = t("gath", [P, 2, GU, FW])
        hot = t("hot", [P, 2, GU, P])
        hotT = t("hotT", [P, 2, BLK * P])
        er_all = t("er_all", [P, GU * RELS * HEADS])
        er_e = t("er_e", [P, GU, HEADS])
        e_sb = t("e_sb", [P, 2, P])
        seg = t("seg", [P, 2, UNIT])
        dn = t("dn", [P, UNIT])
        spread = t("spread", [P, 5, GU])
        lv = t("lv", [HEADS, 8, GU + 1])
        yz = t("yz", [HEADS, 2, GU])
        first_hot = t("first_hot", [HEADS, P])
        phi_log = t("phi_log", [HEADS, 1])
        phi_diag = t("phi_diag", [HEADS, HEADS])
        yz_all = t("yz_all", [P, 2, GU])
        yz_col = t("yz_col", [P, 2])
        phi = t("phi", [P, HEADS])
        psM = psum("psM", [P, 512])
        psOT = psum("psOT", [P, 2, 512])
        psE = psum("psE", [P, 2, 512])
        psS = psum("psS", [P, 512])
        psP = psum("psP", [P, 2, 512])
        CREDIT = 2 * GB + 2
        S_ET, S_LV, S_YZ, S_PHI, S_DT = 0, 128, 288, 352, 356

        meta_in = [sem("meta_in0"), sem("meta_in1")]
        gath_in = [sem("gath_in0"), sem("gath_in1")]
        col_ready, rows_ready, rowsT_ready, idx_ready = sem("col_ready"), sem("rows_ready"), sem("rowsT_ready"), sem("idx_ready")
        hot_ready, hotT_ready, hotT_copied, er_done = sem("hot_ready"), sem("hotT_ready"), sem("hotT_copied"), sem("er_done")
        e_ready, eT_ready, spread_ready, lv_ready = sem("e_ready"), sem("eT_ready"), sem("spread_ready"), sem("lv_ready")
        yz_ready, yzT_ready, dn_ready, dnT_ready = sem("yz_ready"), sem("yzT_ready"), sem("dn_ready"), sem("dnT_ready")
        exp_ready, scaled, sum_ready, sum_used = sem("exp_ready"), sem("scaled"), sem("sum_ready"), sem("sum_used")
        squared = sem("squared")
        v_step = sem("v_step_edges")
        carrier = sem("carrier")
        edge_rows = edges.rearrange("t c e -> t (c e)")

        def each_group(eng, body, first=0):
            loops = (GROUPS - 2 - first) // 2
            with eng.Fori(0, loops) as i:
                for k in range(2):
                    body(i * 2 + (first + k), (first + k) % 2, True, True)
            for g in range(first + 2 * loops, GROUPS):
                body(g, g % 2, g + 1 < GROUPS, g + 2 < GROUPS)

        def each_period(eng, body):
            body(0, 0, False, True, True)
            each_group(eng, lambda g, q, has_next, has_after: body(g, q, True, has_next, has_after), first=1)

        with nc.Block() as block:
            @block.gpsimd
            def _(pool):
                def gather_meta(g, q):
                    pool.tensor_copy(row_col[:, q:q + 1], sb["row_of"][:, bass.ds(g, 1)]).then_inc(col_ready, 1)
                    wait_apart(pool, col_ready, g + 1, carrier)
                    pool.indirect_dma_start(meta[:, q], None, edge_rows,
                                            bass.IndirectOffsetOnAxis(ap=row_col[:, q:q + 1], axis=0)).then_inc(meta_in[q], 16)

                def gather_features(g, q, reuse=False):
                    wait_apart(pool, idx_ready, g + 1, carrier)
                    for u in range(GU):
                        if reuse and u % BLK == 0:
                            wait_apart(pool, sum_ready, g * GB - 2 * GB + u // BLK + 1, carrier)
                        pool.indirect_dma_start(gath[:, q, u], None, feats,
                                                bass.IndirectOffsetOnAxis(ap=idxT[:, q, u:u + 1], axis=0)).then_inc(gath_in[q], 16)

                gather_meta(0, 0)
                gather_meta(1, 1)
                gather_features(0, 0)
                gather_meta(2, 0)
                gather_features(1, 1)

                def group(g, q, has_next, has_after):
                    if has_next:
                        gather_meta(g + 1, 1 - q)
                    gather_features(g, q, reuse=True)

                each_group(pool, group, first=2)

            @block.vector
            def _(dve):
                step = Chain(dve, v_step)
                K_GROUP = 30

                def meta_rows(g, q):
                    tiles = sb["tile_of"][:, bass.ds(g, 1)]
                    dve.tensor_copy(tile_col[:, 0:1], tiles)
                    step(dve.tensor_scalar(tile_col[:, 1:2], tiles, -float(P), None, ALU.mult))
                    dve.wait_ge(meta_in[q], 8 * g + 16 - 8 * q)
                    dst, src, typ = (meta[:, q, k * UNIT:(k + 1) * UNIT] for k in range(3))
                    dve.scalar_tensor_tensor(rows[:, 0], src, float(RELS), typ, ALU.mult, ALU.add)
                    dve.tensor_copy(rows[:, 2], typ)
                    dve.tensor_scalar(rows[:, 1], dst, tile_col[:, 1:2], None, ALU.add).then_inc(rows_ready, 1)
                    dve.wait_ge(rows_ready, g + 1)
                    dve.tensor_scalar(cat[:, q, 2:4], rows[:, 1, 0:UNIT:UNIT - 1], 64.0, tile_col[:, 0:1], ALU.mult, ALU.add)
                    dve.tensor_copy(cat[:, q, 4:5], rows[:, 1, 0:1])
                    dve.memset(reset[:, q, 0:UNIT + 1:UNIT], 0.0)
                    step(dve.tensor_tensor(reset[:, q, 1:UNIT], rows[:, 1, 1:UNIT], rows[:, 1, 0:UNIT - 1], ALU.not_equal))
                    dve.tensor_scalar(reset[:, q, 1:UNIT], reset[:, q, 1:UNIT], -BIG, None, ALU.mult)
                    dve.wait_ge(rowsT_ready, g + 1)
                    dve.tensor_copy(idxT[:, q], psM[:, 0:P:HEADS])
                    dve.tensor_scalar(ndlT[:, q], psM[:, P:2 * P:HEADS], -1.0, None, ALU.mult).then_inc(idx_ready, 1)
                    step(dve.tensor_tensor(typeT[:, q], psM[:, 2 * P:3 * P:HEADS].unsqueeze(2).to_broadcast([P, GU, RELS]),
                                           iota8.unsqueeze(1).to_broadcast([P, GU, RELS]), ALU.is_equal))

                def pick_right(g, q):
                    dve.wait_ge(er_done, GB * g + GB)
                    all4 = er_all[:].rearrange("p (u r h) -> p u r h", u=GU, r=RELS)
                    step(dve.tensor_tensor(all4, psE[:].rearrange("p b (u r h) -> p (b u) r h", r=RELS, h=HEADS),
                                           typeT[:, q].unsqueeze(3).to_broadcast([P, GU, RELS, HEADS]), ALU.mult))
                    step(dve.tensor_reduce(er_e[:], all4.rearrange("p u r h -> p u h r"), AX.X, ALU.add))

                def logits(g, q):
                    dve.wait_ge(gath_in[q], 256 * g + 512 - 256 * q)
                    e0 = e_sb[:, 0].rearrange("p (u h) -> p u h", h=HEADS)
                    step(dve.tensor_tensor(e0, gath[:, q, :, D:FW], er_e[:], ALU.add))
                    dve.scalar_tensor_tensor(e_sb[:, 1], e_sb[:, 0], SLOPE, e_sb[:, 0], ALU.mult, ALU.max).then_inc(e_ready, 1)

                def chunk_maxima(g, q):
                    fwd, bwd = reset[:, q, 0:UNIT], reset[:, q, UNIT:0:-1]
                    dve.wait_ge(eT_ready, g + 1)
                    step(dve.tensor_tensor_scan(seg[:, 0], fwd, psS[:, S_ET:S_ET + UNIT], -BIG, ALU.add, ALU.max))
                    step(dve.tensor_tensor_scan(seg[:, 1, ::-1], bwd, seg[:, 0, ::-1], -BIG, ALU.add, ALU.max))
                    step(dve.tensor_copy(cat[:, q, 0:2], seg[:, 1, 0:UNIT:UNIT - 1]))
                    dve.tensor_tensor(spread[:], cat[:, q].unsqueeze(2).to_broadcast([P, 5, GU]),
                                      masku.unsqueeze(1).to_broadcast([P, 5, GU]), ALU.mult).then_inc(spread_ready, 1)

                def chain_maxima(g, q):
                    lf, ll, kf, kl, fp = (psS[0:HEADS, S_LV + k * GU:S_LV + (k + 1) * GU] for k in range(5))
                    k_last, r_last = lv[:, 0], lv[:, 1]
                    go_on, no_go, single, both, m_first, tail = (lv[:, k] for k in range(2, 8))
                    dve.wait_ge(lv_ready, g + 1)
                    step(dve.tensor_copy(k_last[:, 1:GU + 1], kl))
                    dve.tensor_scalar(first_hot[:], iota[0:HEADS, :], fp[:, 0:1], None, ALU.is_equal)
                    step(dve.tensor_tensor(go_on[:, 0:GU], kf, k_last[:, 0:GU], ALU.is_equal))
                    dve.tensor_tensor(single[:, 0:GU], kf, k_last[:, 1:GU + 1], ALU.is_equal)
                    step(dve.tensor_scalar(no_go[:, 0:GU], go_on[:, 0:GU], 1.0, BIG, ALU.subtract, ALU.mult))
                    step(dve.tensor_scalar(single[:, 0:GU], single[:, 0:GU], 1.0, BIG, ALU.subtract, ALU.mult))
                    step(dve.tensor_tensor(both[:, 0:GU], no_go[:, 0:GU], single[:, 0:GU], ALU.min))
                    step(dve.tensor_tensor_scan(r_last[:, 1:GU + 1], both[:, 0:GU], ll, r_last[:, 0:1], ALU.add, ALU.max))
                    step(dve.tensor_tensor(m_first[:, 0:GU], r_last[:, 0:GU], no_go[:, 0:GU], ALU.add))
                    step(dve.tensor_tensor(m_first[:, 0:GU], m_first[:, 0:GU], lf, ALU.max))
                    dve.tensor_copy(tail[:, GU - 1:GU], r_last[:, GU:GU + 1])
                    step(dve.tensor_tensor(tail[:, 0:GU - 1], m_first[:, 1:GU], no_go[:, 1:GU], ALU.add))
                    step(dve.tensor_tensor(tail[:, 0:GU - 1], tail[:, 0:GU - 1], r_last[:, 1:GU], ALU.max))
                    step(dve.tensor_tensor_scan(yz[:, 1, ::-1], both[:, GU:0:-1], tail[:, GU - 1::-1], -BIG, ALU.add, ALU.max))
                    step(dve.tensor_tensor(yz[:, 0], yz[:, 1], single[:, 0:GU], ALU.add))
                    step(dve.tensor_tensor(yz[:, 0], yz[:, 0], m_first[:, 0:GU], ALU.max))
                    step(dve.tensor_tensor(phi_log[:], r_last[:, 0:1], yz[:, 0, 0:1], ALU.subtract))
                    step(dve.tensor_tensor(phi_log[:], phi_log[:], go_on[:, 0:1], ALU.mult))
                    dve.tensor_scalar(phi_diag[:], ident[0:HEADS, 0:HEADS], phi_log[:], None, ALU.mult).then_inc(yz_ready, 1)
                    dve.tensor_copy(k_last[:, 0:1], k_last[:, GU:GU + 1])
                    step(dve.tensor_copy(r_last[:, 0:1], r_last[:, GU:GU + 1]))

                def shifts(g, q):
                    fwd, bwd = reset[:, q, 0:UNIT], reset[:, q, UNIT:0:-1]
                    dve.wait_ge(yzT_ready, g + 1)
                    step(dve.tensor_tensor(yz_all[:], psS[:, S_YZ:S_YZ + 2 * GU].rearrange("p (y u) -> p y u", y=2),
                                           masku.unsqueeze(1).to_broadcast([P, 2, GU]), ALU.mult))
                    step(dve.tensor_reduce(yz_col[:], yz_all[:], AX.X, ALU.add))
                    step(dve.tensor_tensor_scan(seg[:, 0], fwd, seg[:, 1], yz_col[:, 0:1], ALU.add, ALU.max))
                    step(dve.tensor_tensor_scan(seg[:, 1, ::-1], bwd, seg[:, 0, ::-1], yz_col[:, 1:2], ALU.add, ALU.max))
                    dve.tensor_tensor(dn[:], psS[:, S_ET:S_ET + UNIT], seg[:, 1], ALU.subtract).then_inc(dn_ready, 1)

                def tile_acc(g, b):
                    d = dve.value_load(pair_tile[0:1, bass.ds(g, 1), b], min_val=0, max_val=TILES - 1)
                    return acc[:, bass.ds(d, 1), :].rearrange("p a w -> p (a w)")

                def scale(g, q, b):
                    rows_b = gath[:, q, b * BLK:(b + 1) * BLK]
                    feat = rows_b[:, :, 0:D].rearrange("p u (h d) -> p u h d", h=HEADS)
                    dve.tensor_tensor(feat, feat, rows_b[:, :, D:FW].unsqueeze(3).to_broadcast([P, BLK, HEADS, HD]),
                                      ALU.mult).then_inc(scaled, 1)

                def add(g, b, into=None):
                    into = tile_acc(g, b) if into is None else into
                    dve.wait_ge(sum_ready, GB * g + b + 1)
                    dve.tensor_tensor(into, into, psP[:, b % 2, 0:FW], ALU.add).then_inc(sum_used, 1)
                    dve.wait_ge(sum_used, GB * g + b + 1 + CREDIT)

                dve.sem_inc(sum_used, CREDIT)
                dve.memset(lv[:, 0, 0:1], -1.0)
                step(dve.memset(lv[:, 1, 0:1], -BIG))
                step(dve.memset(lv[:, 5, GU:GU + 1], 0.0))
                meta_rows(0, 0)
                meta_rows(1, 1)
                pick_right(0, 0)
                start = []

                def period(g, q, has_prev, has_next, has_after):
                    if has_prev and not start:
                        start.append(step.n)
                    if has_prev and len(start) == 1:
                        step.start((g - 1) * K_GROUP + start[0])
                        if not has_after:
                            start.append(g)
                    logits(g, q)
                    if has_prev:
                        scale(g - 1, 1 - q, 6)
                    chunk_maxima(g, q)
                    if has_prev:
                        scale(g - 1, 1 - q, 7)
                        add(g - 1, 4)
                    chain_maxima(g, q)
                    if has_prev:
                        add(g - 1, 5)
                    shifts(g, q)
                    if has_prev:
                        add(g - 1, 6)
                        add(g - 1, 7)
                    into = tile_acc(g, 0)
                    dve.wait_ge(exp_ready, g + 1)
                    scale(g, q, 0)
                    scale(g, q, 1)
                    dve.tensor_tensor(into[:, D:FW], into[:, D:FW], phi[:], ALU.mult)
                    feat = into[:, 0:D].rearrange("p (h d) -> p h d", h=HEADS)
                    step(dve.tensor_tensor(feat, feat, phi[:].unsqueeze(2).to_broadcast([P, HEADS, HD]), ALU.mult))
                    for b in range(GB // 2):
                        scale(g, q, b + 2)
                        add(g, b, into if b == 0 else None)
                    if has_after:
                        meta_rows(g + 2, q)
                    if has_next:
                        pick_right(g + 1, 1 - q)
                    if has_prev and has_after:
                        assert step.n == K_GROUP or len(start) == 2, step.n

                each_period(dve, period)
                last, q = GROUPS - 1, (GROUPS - 1) % 2
                scale(last, q, 6)
                add(last, 4)
                scale(last, q, 7)
                for b in range(5, GB):
                    add(last, b)

            @block.scalar
            def _(act):
                def one_hot(n, q, b):
                    if b == 0:
                        act.wait_ge(idx_ready, n + 1)
                    act.wait_ge(sum_used, GB * n + b + 1 + CREDIT - 2 * GB)
                    for k in range(BLK):
                        u = b * BLK + k
                        ins = act.activation(square[:, b % 2, k], iota, ACT.Square, bias=ndlT[:, q, u:u + 1])
                    ins.then_inc(squared, 1)
                    act.wait_ge(squared, GB * n + b + 1)
                    act.activation(hot[:, q, b * BLK:(b + 1) * BLK], square[:, b % 2], ACT.Relu, bias=1.0,
                                   scale=-1.0).then_inc(hot_ready, 1)

                def copy(n, b):
                    act.wait_ge(hotT_ready, GB * n + b + 1)
                    act.copy(hotT[:, b % 2], psOT[:, b % 2]).then_inc(hotT_copied, 1)

                def both(n, q, pairs):
                    for b in pairs:
                        one_hot(n, q, b)
                        if b:
                            copy(n, b - 1)

                both(0, 0, range(GB))
                copy(0, GB - 1)

                def period(g, q, has_prev, has_next, has_after):
                    if has_next:
                        both(g + 1, 1 - q, range(3))
                        one_hot(g + 1, 1 - q, 3)
                    act.wait_ge(dnT_ready, g + 1)
                    act.activation(phi[:], psS[:, S_PHI:S_PHI + HEADS], ACT.Exp)
                    act.activation(gath[:, q, :, D:FW], psS[:, S_DT:S_DT + P].rearrange("p (u h) -> p u h", h=HEADS),
                                   ACT.Exp).then_inc(exp_ready, 1)
                    if has_next:
                        copy(g + 1, 2)
                        both(g + 1, 1 - q, range(4, GB))
                        copy(g + 1, GB - 1)

                each_period(act, period)

            @block.tensor
            def _(pe):
                def meta_rows(g):
                    pe.wait_ge(rows_ready, g + 1)
                    for k in range(3):
                        ins = pe.transpose(psM[:, k * P:(k + 1) * P], rows[:, k], ident)
                    ins.then_inc(rowsT_ready, 1)

                def turn(n, q, b):
                    pe.wait_ge(hot_ready, GB * n + b + 1)
                    for k in range(BLK):
                        ins = pe.transpose(psOT[:, b % 2, k * P:(k + 1) * P], hot[:, q, b * BLK + k], ident)
                    ins.then_inc(hotT_ready, 1)

                def right_logits(n, b):
                    d = pe.value_load(pair_tile[0:1, bass.ds(n, 1), b], min_val=0, max_val=TILES - 1)
                    table = er_sb[:, bass.ds(d, 1), :].rearrange("p a c -> p (a c)")
                    pe.wait_ge(hotT_copied, GB * n + b + 1)
                    W = RELS * HEADS
                    for k in range(BLK):
                        at = ((b * BLK + k) * W) % 512
                        ins = pe.matmul(psE[:, b // 4, at:at + W], hotT[:, b % 2, k * P:(k + 1) * P], table,
                                        start=True, stop=True)
                    ins.then_inc(er_done, 1)

                def prepare(n, q, b):
                    turn(n, q, b)
                    if b:
                        right_logits(n, b - 1)
                    if b == GB - 1:
                        right_logits(n, b)

                meta_rows(0)
                meta_rows(1)
                for b in range(GB):
                    prepare(0, 0, b)

                def total(g, q, b):
                    pe.wait_ge(scaled, GB * g + b + 1)
                    pe.wait_ge(sum_used, GB * g + b - 1 + CREDIT)
                    for k in range(BLK):
                        ins = pe.matmul(psP[:, b % 2, 0:FW], hot[:, q, b * BLK + k], gath[:, q, b * BLK + k],
                                        start=k == 0, stop=k == BLK - 1)
                    ins.then_inc(sum_ready, 1)

                def period(g, q, has_prev, has_next, has_after):
                    def ahead(b):
                        if has_next:
                            prepare(g + 1, 1 - q, b)

                    def behind(b):
                        if has_prev:
                            total(g - 1, 1 - q, b)

                    pe.wait_ge(e_ready, g + 1)
                    pe.transpose(psS[:, S_ET:S_ET + P], e_sb[:, 1], ident).then_inc(eT_ready, 1)
                    behind(4)
                    pe.wait_ge(spread_ready, g + 1)
                    pe.matmul(psS[0:HEADS, S_LV:S_LV + 5 * GU], selh, spread[:].rearrange("p k u -> p (k u)"),
                              start=True, stop=True).then_inc(lv_ready, 1)
                    behind(5)
                    ahead(0)
                    ahead(1)
                    pe.wait_ge(yz_ready, g + 1)
                    pe.matmul(psS[:, S_PHI:S_PHI + HEADS], first_hot[:], phi_diag[:], start=True, stop=True)
                    pe.matmul(psS[:, S_YZ:S_YZ + 2 * GU], selht, yz[:].rearrange("p y u -> p (y u)"),
                              start=True, stop=True).then_inc(yzT_ready, 1)
                    behind(6)
                    pe.wait_ge(dn_ready, g + 1)
                    pe.transpose(psS[:, S_DT:S_DT + P], dn[:], ident).then_inc(dnT_ready, 1)
                    behind(7)
                    ahead(2)
                    total(g, q, 0)
                    ahead(3)
                    total(g, q, 1)
                    ahead(4)
                    total(g, q, 2)
                    ahead(5)
                    total(g, q, 3)
                    if has_after:
                        meta_rows(g + 2)
                    ahead(6)
                    ahead(7)

                each_period(pe, period)
                for b in range(4, GB):
                    total(GROUPS - 1, (GROUPS - 1) % 2, b)


def route_stage(nc, sb, bias, wr, br, slots_x):
    with ExitStack() as ctx:
        def t(name, shape, dt=F32):
            return ctx.enter_context(nc.sbuf_tensor(name, shape, dt))

        def sem(name):
            return ctx.enter_context(nc.semaphore(name))

        TE = TILES * EXPERTS
        cst, acc, xs, slot_i, weight = sb["cst"], sb["acc"], sb["xs"], sb["slot_i"], sb["weight"]
        ident = cst[:, C_ID:C_ID + P]
        bias_all = t("bias_all", [P, D])
        wr_sb = t("wr_sb", [P, KD, EXPERTS])
        br_all = t("br_all", [P, EXPERTS])
        rden = t("rden", [P, TILES, HEADS])
        stats = t("stats_r", [P, TILES, 6])
        mean = t("mean_r", [P, TILES])
        std = t("std_r", [P, TILES])
        rstd = t("rstd_r", [P, TILES])
        eps = t("eps_r", [P, 1])
        ones = t("ones_r", [P, P])
        xt = t("xt", [P, TILES, D])
        xtT = t("xtT", [P, 2, KD, P])
        prob = t("prob", [P, TILES, EXPERTS])
        left = t("left", [P, TILES, EXPERTS])
        work = t("work", [P, TILES, EXPERTS])
        hot1 = t("hot1", [P, TILES, EXPERTS])
        hot2 = t("hot2", [P, TILES, EXPERTS])
        top = t("top", [P, 2, TILES])
        col = t("col", [P, TILES])
        mask = t("mask", [P, EXPERTS, TILES])
        keep = t("keep", [P, EXPERTS, TILES])
        upto = t("upto", [P, EXPERTS, TILES])
        place = t("place", [P, EXPERTS, TILES])
        need_i = t("need_i", [P, EXPERTS], I32)
        need = t("need", [P, EXPERTS])
        ends = t("ends", [P, EXPERTS])
        base = t("base", [P, EXPERTS])
        slot_f = t("slot_f", [P, 2, TILES])
        done = t("done", [1, SLOT_TILES, EXPERTS])
        owner = t("owner", [1, SLOT_TILES])
        xn = t("xn", [P, 2, D])
        slot_col = t("slot_col", [P, 2, 2], I32)
        psT = ctx.enter_context(nc.psum_tensor("psT_r", [P, 2, 512], F32))
        psL = ctx.enter_context(nc.psum_tensor("psL", [P, 512], F32))
        psC = ctx.enter_context(nc.psum_tensor("psC_r", [P, 2, 512], F32))
        small_in = sem("small_in")
        v_step = sem("v_step_route")
        var_ready, std_ready = sem("var_ready_r"), sem("std_ready_r")
        xt_ready, xtT_ready, xtT_copied = sem("xt_ready"), sem("xtT_ready"), sem("xtT_copied")
        logits_ready, shifted, exped = sem("logits_ready"), sem("shifted"), sem("exped")
        mask_ready, counted = sem("mask_ready"), sem("counted_r")
        xn_ready = sem("xn_ready")
        carrier = sem("carrier_r")
        scattered = [sem("scattered0"), sem("scattered1")]

        def tile(ap, i):
            return ap[:, bass.ds(i, 1), :].rearrange("p a f -> p (a f)")

        with nc.Block() as block:
            @block.sync
            def _(sp):
                sp.dma_start(bias_all[:], bias.to_broadcast([P, D])).then_inc(small_in, 16)
                sp.dma_start(wr_sb[:], wr.rearrange("(k p) e -> p k e", p=P)).then_inc(small_in, 16)
                sp.dma_start(br_all[:], br.to_broadcast([P, EXPERTS])).then_inc(small_in, 16)

            @block.scalar
            def _(act):
                act.wait_ge(var_ready, 1)
                act.activation(std[:], std[:], ACT.Sqrt, bias=eps[:]).then_inc(std_ready, 1)
                with act.Fori(0, TILES // 2) as i:
                    for q in range(2):
                        act.wait_ge(xtT_ready, i * 2 + q + 1)
                        act.copy(xtT[:, q].rearrange("p k c -> p (k c)"), psT[:, q, 0:D]).then_inc(xtT_copied, 1)
                act.wait_ge(var_ready, 2)
                act.activation(std[:], std[:], ACT.Sqrt, bias=eps[:]).then_inc(std_ready, 1)
                act.wait_ge(shifted, 1)
                act.activation(prob[:], prob[:], ACT.Exp).then_inc(exped, 1)

            @block.tensor
            def _(pe):
                pe.wait_ge(small_in, 48)
                for i in range(TILES):
                    pe.wait_ge(xt_ready, i + 1)
                    if i >= 2:
                        pe.wait_ge(xtT_copied, i - 1)
                    for k in range(KD):
                        ins = pe.transpose(psT[:, i % 2, k * P:(k + 1) * P], xt[:, i, k * P:(k + 1) * P], ident)
                    ins.then_inc(xtT_ready, 1)
                    for j in ([i - 1] if i >= 1 else []) + ([i] if i == TILES - 1 else []):
                        pe.wait_ge(xtT_copied, j + 1)
                        for k in range(KD):
                            ins = pe.matmul(psL[:, j * EXPERTS:(j + 1) * EXPERTS], xtT[:, j % 2, k], wr_sb[:, k],
                                            start=k == 0, stop=k == KD - 1)
                ins.then_inc(logits_ready, 1)
                pe.wait_ge(mask_ready, 1)
                counts = mask[:].rearrange("p e t -> p (e t)")
                pe.matmul(psC[:, 0, 0:TE], cst[:, C_TRI:C_TRI + P], counts, start=True, stop=True)
                pe.matmul(psC[:, 1, 0:TE], ones[:], counts, start=True, stop=True).then_inc(counted, 1)

            @block.vector
            def _(dve):
                step = Chain(dve, v_step)

                def norms(of, n):
                    with dve.Fori(0, TILES) as i:
                        dve.bn_stats(tile(stats, i), tile(of, i)).then_inc(v_step, 1)
                    dve.wait_ge(v_step, step.n + TILES)
                    step.n += TILES
                    mean_var(dve, step, stats, mean[:], std[:])
                    dve.sem_inc(var_ready, 1)
                    dve.wait_ge(std_ready, n)
                    step(dve.reciprocal(rstd[:], std[:]))

                step(dve.memset(eps[:], EPS))
                dve.memset(ones[:], 1.0)
                step(dve.memset(keep[:], 1.0))
                step(dve.memset(keep[:, :, 0:1], 0.0))
                step(dve.tensor_scalar(rden[:], acc[:, :, D:FW], 1e-30, None, ALU.max))
                step(dve.reciprocal(rden[:], rden[:]))
                dve.wait_ge(small_in, 48)
                for h in range(HEADS):
                    part = acc[:, :, h * HD:(h + 1) * HD]
                    ins = dve.tensor_tensor(part, part, rden[:, :, h:h + 1].to_broadcast([P, TILES, HD]), ALU.mult)
                step(ins)
                step(dve.tensor_tensor(acc[:, :, 0:D], acc[:, :, 0:D], bias_all[:].unsqueeze(1).to_broadcast([P, TILES, D]), ALU.add))
                step(dve.tensor_tensor(xs[:], xs[:], acc[:, :, 0:D], ALU.add))
                norms(xs, 1)
                with dve.Fori(0, TILES) as i:
                    dve.tensor_scalar(tile(xt, i), tile(xs, i), mean[:, bass.ds(i, 1)], rstd[:, bass.ds(i, 1)],
                                      ALU.subtract, ALU.mult).then_inc(xt_ready, 1)
                dve.wait_ge(xt_ready, TILES)
                norms(xt, 2)
                per = [P, TILES, EXPERTS]
                dve.wait_ge(logits_ready, 1)
                step(dve.tensor_tensor(prob[:], psL[:, 0:TE].rearrange("p (t e) -> p t e", e=EXPERTS),
                                       br_all[:].unsqueeze(1).to_broadcast(per), ALU.add))
                step(dve.tensor_reduce(col[:], prob[:], AX.X, ALU.max))
                step(dve.tensor_tensor(prob[:], prob[:], col[:].unsqueeze(2).to_broadcast(per), ALU.subtract))
                dve.sem_inc(shifted, 1)
                dve.wait_ge(exped, 1)
                step(dve.tensor_reduce(col[:], prob[:], AX.X, ALU.add))
                step(dve.reciprocal(col[:], col[:]))
                step(dve.tensor_tensor(prob[:], prob[:], col[:].unsqueeze(2).to_broadcast(per), ALU.mult))
                iota = cst[:, C_IOTA8:C_IOTA8 + EXPERTS].unsqueeze(1).to_broadcast(per)
                for k, (of, hot) in enumerate(((prob, hot1), (left, hot2))):
                    step(dve.tensor_reduce(top[:, k], of[:], AX.X, ALU.max))
                    step(dve.tensor_tensor(work[:], of[:], top[:, k].unsqueeze(2).to_broadcast(per), ALU.not_equal))
                    step(dve.scalar_tensor_tensor(work[:], work[:], float(EXPERTS), iota, ALU.mult, ALU.add))
                    step(dve.tensor_reduce(col[:], work[:], AX.X, ALU.min))
                    step(dve.tensor_tensor(hot[:], iota, col[:].unsqueeze(2).to_broadcast(per), ALU.is_equal))
                    if k == 0:
                        step(dve.scalar_tensor_tensor(left[:], hot1[:], -2.0, prob[:], ALU.mult, ALU.add))
                step(dve.tensor_tensor(col[:], top[:, 0], top[:, 1], ALU.add))
                step(dve.reciprocal(col[:], col[:]))
                dve.tensor_tensor(weight[:], top[:], col[:].unsqueeze(1).to_broadcast([P, 2, TILES]), ALU.mult)
                step(dve.tensor_tensor(mask[:], hot1[:].rearrange("p t e -> p e t"), hot2[:].rearrange("p t e -> p e t"), ALU.add))
                dve.sem_inc(mask_ready, 1)
                dve.wait_ge(counted, 1)
                flat = "p e t -> p (e t)"
                step(dve.tensor_tensor_scan(upto[:].rearrange(flat), keep[:].rearrange(flat), psC[:, 1, 0:TE], 0.0, ALU.mult, ALU.add))
                step(dve.tensor_scalar(need[:], upto[:, :, TILES - 1], float(SLOT_TILE - 1), None, ALU.add))
                step(dve.tensor_copy(need_i[:], need[:]))
                step(dve.tensor_scalar(need_i[:], need_i[:], SLOT_TILE.bit_length() - 1, None, ALU.arith_shift_right))
                step(dve.tensor_copy(need[:], need_i[:]))
                step(dve.tensor_scalar(need[:], need[:], float(SLOT_TILE), None, ALU.mult))
                step(dve.tensor_tensor_scan(ends[:], ones[:, 0:EXPERTS], need[:], 0.0, ALU.mult, ALU.add))
                step(dve.tensor_tensor(base[:], ends[:], need[:], ALU.subtract))
                step(dve.tensor_tensor(place[:].rearrange(flat), upto[:].rearrange(flat), psC[:, 1, 0:TE], ALU.subtract))
                step(dve.tensor_tensor(place[:].rearrange(flat), place[:].rearrange(flat), psC[:, 0, 0:TE], ALU.add))
                step(dve.tensor_tensor(place[:], place[:], base[:].unsqueeze(2).to_broadcast([P, EXPERTS, TILES]), ALU.add))
                for k, hot in enumerate((hot1, hot2)):
                    step(dve.tensor_tensor(work[:], hot[:], place[:].rearrange("p e t -> p t e"), ALU.mult))
                    step(dve.tensor_reduce(slot_f[:, k], work[:], AX.X, ALU.add))
                step(dve.tensor_copy(slot_i[:], slot_f[:]))
                step(dve.tensor_tensor(done[:], ends[0:1].unsqueeze(1).to_broadcast([1, SLOT_TILES, EXPERTS]),
                                       cst[0:1, C_SLOT:C_SLOT + SLOT_TILES].unsqueeze(2).to_broadcast([1, SLOT_TILES, EXPERTS]), ALU.is_le))
                step(dve.tensor_reduce(owner[:], done[:], AX.X, ALU.add))
                step(dve.tensor_scalar(owner[:], owner[:], float(EXPERTS - 1), None, ALU.min))
                step(dve.tensor_copy(sb["expert_of"][:], owner[:]))
                def to_send(at, q):
                    dve.tensor_copy(slot_col[:, q], slot_i[:, :, bass.ds(at, 1)].rearrange("p k a -> p (k a)"))
                    dve.tensor_scalar(xn[:, q], tile(xt, at), mean[:, bass.ds(at, 1)], rstd[:, bass.ds(at, 1)],
                                      ALU.subtract, ALU.mult).then_inc(xn_ready, 1)

                to_send(0, 0)
                to_send(1, 1)
                with dve.Fori(1, TILES // 2) as i:
                    for q in range(2):
                        dve.wait_ge(scattered[q], i * 32)
                        to_send(i * 2 + q, q)

            @block.gpsimd
            def _(pool):
                with pool.Fori(0, TILES // 2) as i:
                    for q in range(2):
                        wait_apart(pool, xn_ready, i * 2 + q + 1, carrier)
                        for k in range(2):
                            pool.indirect_dma_start(slots_x, bass.IndirectOffsetOnAxis(ap=slot_col[:, q, k:k + 1], axis=0),
                                                    xn[:, q], None).then_inc(scattered[q], 16)
                for q in range(2):
                    pool.wait_ge(scattered[q], 32 * (TILES // 2))


def expert_stage(nc, sb, experts, b2, slots_x, slots_y):
    with ExitStack() as ctx:
        def t(name, shape, dt=F32):
            return ctx.enter_context(nc.sbuf_tensor(name, shape, dt))

        def sem(name):
            return ctx.enter_context(nc.semaphore(name))

        HALVES = SLOT_TILE // P
        ident = sb["cst"][:, C_ID:C_ID + P]
        wbuf = t("wbuf", [P, 2, E_W])
        b2_all = t("b2_all", [P, 2, D])
        xrow = t("xrow", [P, 2, HALVES, D])
        xeT = t("xeT", [P, 2, KD, SLOT_TILE])
        hT = t("hT", [P, KH, SLOT_TILE])
        yrow = t("yrow", [P, 2, HALVES, D])
        psX = ctx.enter_context(nc.psum_tensor("psX", [P, 2, 512], F32))
        psH = ctx.enter_context(nc.psum_tensor("psH", [P, 2, 512], F32))
        psY = ctx.enter_context(nc.psum_tensor("psY", [P, HALVES, 512], F32))
        w_in = [sem("w_in0"), sem("w_in1")]
        x_in = [sem("x_in0"), sem("x_in1")]
        y_stored = [sem("y_stored0"), sem("y_stored1")]
        xT_ready, xe_ready = sem("xT_ready_e"), sem("xe_ready")
        h_ready, h_used, gelu_done = sem("h_ready"), sem("h_used"), sem("gelu_done")
        y_ready, y_copied = sem("y_ready"), sem("y_copied")
        tile_done = sem("tile_done")

        def w1(q, k, m):
            return wbuf[:, q, k * HID + m * P:k * HID + (m + 1) * P]

        def w2(q, m):
            return wbuf[:, q, E_W2 + m * D:E_W2 + (m + 1) * D]

        def each_tile(eng, body, last_too=True):
            with eng.Fori(0, (SLOT_TILES - 1) // 2) as i:
                body(i * 2, 0, False)
                body(i * 2 + 1, 1, False)
            body(SLOT_TILES - 1, 0, True)
        assert SLOT_TILES % 2 == 1

        with nc.Block() as block:
            @block.sync
            def _(sp):
                def load(s, q):
                    e = sp.value_load(sb["expert_of"][0:1, bass.ds(s, 1)], min_val=0, max_val=EXPERTS - 1)
                    sp.dma_start(wbuf[:, q], experts[bass.ds(e * P, P), :]).then_inc(w_in[q], 16)
                    sp.dma_start(b2_all[:, q], b2[bass.ds(e, 1), :].to_broadcast([P, D])).then_inc(w_in[q], 16)
                    sp.dma_start(xrow[:, q], slots_x[bass.ds(s * SLOT_TILE, SLOT_TILE), :].rearrange(
                        "(j p) f -> p j f", p=P)).then_inc(x_in[q], 16)

                load(0, 0)
                sp.sem_inc(tile_done, 1)

                def body(s, q, last):
                    if not last:
                        sp.wait_ge(tile_done, s + 1)
                        load(s + 1, 1 - q)
                    sp.wait_ge(y_copied, s * HALVES + 2 * HALVES)
                    sp.dma_start(slots_y[bass.ds(s * SLOT_TILE, SLOT_TILE), :].rearrange("(j p) f -> p j f", p=P),
                                 yrow[:, q]).then_inc(y_stored[q], 16)

                each_tile(sp, body)
                sp.wait_ge(y_stored[0], 16 + 16 * (SLOT_TILES // 2 + 1))
                sp.wait_ge(y_stored[1], 16 + 16 * (SLOT_TILES // 2))

            @block.tensor
            def _(pe):
                def turn(s, q):
                    pe.wait_ge(x_in[q], (s - q) * 8 + 16)
                    for k in range(KD):
                        for j in range(HALVES):
                            ins = pe.transpose(psX[:, q, k * SLOT_TILE + j * P:k * SLOT_TILE + (j + 1) * P],
                                               xrow[:, q, j, k * P:(k + 1) * P], ident)
                    ins.then_inc(xT_ready, 1)

                turn(0, 0)

                def body(s, q, last):
                    pe.wait_ge(xe_ready, s + 1)
                    for m in range(KH):
                        if m % 2 == 0:
                            pe.wait_ge(h_used, s * KH + m + 2)
                        for k in range(KD):
                            ins = pe.matmul(psH[:, m // 2 % 2, (m % 2) * SLOT_TILE:(m % 2 + 1) * SLOT_TILE], w1(q, k, m),
                                            xeT[:, q, k], start=k == 0, stop=k == KD - 1)
                        if m % 2:
                            ins.then_inc(h_ready, 1)
                    if not last:
                        turn(s + 1, 1 - q)
                    pe.wait_ge(gelu_done, s + 1)
                    for j in range(HALVES):
                        pe.wait_ge(y_copied, s * HALVES + j + 1)
                        for m in range(KH):
                            ins = pe.matmul(psY[:, j, 0:D], hT[:, m, j * P:(j + 1) * P], w2(q, m),
                                            start=m == 0, stop=m == KH - 1)
                        ins.then_inc(y_ready, 1)

                each_tile(pe, body)

            @block.scalar
            def _(act):
                act.sem_inc(h_used, 4)

                def body(s, q, last):
                    act.wait_ge(xT_ready, s + 1)
                    act.wait_ge(w_in[q], (s - q) * 16 + 32)
                    for k in range(KD):
                        ins = act.activation(xeT[:, q, k], psX[:, q, k * SLOT_TILE:(k + 1) * SLOT_TILE], ACT.Identity,
                                             bias=wbuf[:, q, E_B + k:E_B + k + 1], scale=wbuf[:, q, E_G + k:E_G + k + 1])
                    ins.then_inc(xe_ready, 1)
                    act.wait_ge(y_copied, s * HALVES + HALVES)
                    for m in range(KH):
                        act.wait_ge(h_ready, s * (KH // 2) + m // 2 + 1)
                        act.activation(hT[:, m], psH[:, m // 2 % 2, (m % 2) * SLOT_TILE:(m % 2 + 1) * SLOT_TILE], ACT.Gelu,
                                       bias=wbuf[:, q, E_B1 + m:E_B1 + m + 1]).then_inc(h_used, 1)
                    act.wait_ge(h_used, s * KH + KH + 4)
                    act.sem_inc(gelu_done, 1)

                each_tile(act, body)

            @block.vector
            def _(dve):
                dve.sem_inc(y_copied, HALVES)
                dve.sem_inc(y_stored[0], 16)
                dve.sem_inc(y_stored[1], 16)

                def body(s, q, last):
                    dve.wait_ge(y_stored[q], (s - q) * 8 + 16)
                    for j in range(HALVES):
                        dve.wait_ge(y_ready, s * HALVES + j + 1)
                        dve.tensor_tensor(yrow[:, q, j], psY[:, j, 0:D], b2_all[:, q], ALU.add).then_inc(y_copied, 1)
                    dve.wait_ge(y_copied, s * HALVES + 2 * HALVES)
                    dve.sem_inc(tile_done, 1)

                each_tile(dve, body)


def combine_stage(nc, sb, slots_y, out):
    with ExitStack() as ctx:
        xs, weight = sb["xs"], sb["weight"]
        slot_col = ctx.enter_context(nc.sbuf_tensor("slot_col_c", [P, 4, 2], I32))
        ys = ctx.enter_context(nc.sbuf_tensor("ys", [P, 4, 2, D], F32))
        copied = ctx.enter_context(nc.semaphore("slots_copied"))
        landed = [ctx.enter_context(nc.semaphore(f"y_landed{q}")) for q in range(4)]
        carrier = ctx.enter_context(nc.semaphore("carrier_c"))
        half = ctx.enter_context(nc.semaphore("half_summed"))
        summed = ctx.enter_context(nc.semaphore("summed"))
        stored = ctx.enter_context(nc.semaphore("out_stored"))
        WHOLE = TILES // 2

        with nc.Block() as block:
            @block.gpsimd
            def _(pool):
                with pool.Fori(0, WHOLE) as i:
                    for q in range(2):
                        at = i * 2 + q
                        pool.wait_ge(summed, at + 1)
                        pool.tensor_copy(slot_col[:, q], sb["slot_i"][:, :, bass.ds(at, 1)].rearrange(
                            "p k a -> p (k a)")).then_inc(copied, 1)
                        wait_apart(pool, copied, at + 1, carrier)
                        for k in range(2):
                            pool.indirect_dma_start(ys[:, q, k], None, slots_y, bass.IndirectOffsetOnAxis(
                                ap=slot_col[:, q, k:k + 1], axis=0)).then_inc(landed[q], 16)

            @block.vector
            def _(dve):
                dve.sem_inc(summed, 2)
                with dve.Fori(0, WHOLE) as i:
                    for q in range(2):
                        at = i * 2 + q
                        row = xs[:, bass.ds(at, 1), :].rearrange("p a f -> p (a f)")
                        dve.wait_ge(landed[q], i * 32 + 32)
                        dve.scalar_tensor_tensor(row, ys[:, q, 0], weight[:, 0, bass.ds(at, 1)], row,
                                                 ALU.mult, ALU.add).then_inc(half, 1)
                        dve.wait_ge(half, at + 1)
                        dve.scalar_tensor_tensor(row, ys[:, q, 1], weight[:, 1, bass.ds(at, 1)], row,
                                                 ALU.mult, ALU.add).then_inc(summed, 1)

            @block.sync
            def _(sp):
                with sp.Fori(0, TILES) as i:
                    sp.wait_ge(summed, i + 3)
                    sp.dma_start(out[bass.ds(i * P, P), :], xs[:, bass.ds(i, 1), :].rearrange("p a f -> p (a f)")).then_inc(stored, 16)
                sp.wait_ge(stored, 16 * TILES)


def build(nc, ins, out):
    feats = nc.dram_tensor("feats", (ROWS * RELS, FW), F32, kind="Internal").ap()
    slots_x = nc.dram_tensor("slots_x", (SLOTS, D), F32, kind="Internal").ap()
    slots_y = nc.dram_tensor("slots_y", (SLOTS, D), F32, kind="Internal").ap()
    with ExitStack() as ctx:
        def keep(name, shape, dt=F32):
            return ctx.enter_context(nc.sbuf_tensor(name, shape, dt))

        sb = {
            "cst": keep("cst", [P, C_W]),
            "xs": keep("xs", [P, TILES, D]),
            "er": keep("er", [P, TILES, RELS * HEADS]),
            "acc": keep("acc", [P, TILES, FW]),
            "tile_of": keep("tile_of", [P, GROUPS]),
            "row_of": keep("row_of", [P, GROUPS], I32),
            "pair_tile": keep("pair_tile", [1, GROUPS, GB], I32),
            "slot_i": keep("slot_i", [P, 2, TILES], I32),
            "weight": keep("weight", [P, 2, TILES]),
            "expert_of": keep("expert_of", [1, SLOT_TILES], I32),
        }
        node_stage(nc, sb, ins["x"], ins["conv"], ins["attn_l"], ins["attn_r"], feats, slots_x, ins["consts"])
        schedule_stage(nc, sb, ins["edges"])
        edge_stage(nc, sb, ins["edges"], feats)
        route_stage(nc, sb, ins["bias"], ins["wr"], ins["br"], slots_x)
        expert_stage(nc, sb, ins["experts"], ins["b2"], slots_x, slots_y)
        combine_stage(nc, sb, slots_y, out)


def kernel(x, src, dst, edge_type_8, L0_gnn_conv_weights, L0_gnn_attn_l, L0_gnn_attn_r, L0_gnn_h_bias, L0_ffn_Wr,
           L0_ffn_br, L0_ffn_ln_g, L0_ffn_ln_b, L0_ffn_W1, L0_ffn_b1, L0_ffn_W2, L0_ffn_b2):
    import concourse.bacc as bacc
    from concourse.bass_utils import run_bass_kernel_spmd

    def padded(a, rows, fill=0):
        a = np.asarray(a)
        return np.concatenate([a, np.full((rows - a.shape[0],) + a.shape[1:], fill, a.dtype)])

    def chunks(a, fill):
        return padded(a, CHUNK_ROWS * UNIT, fill).reshape(CHUNK_ROWS, UNIT)

    def columns(a, chunk):
        return np.asarray(a).reshape(EXPERTS, chunk, P).transpose(0, 2, 1)

    w1 = np.asarray(L0_ffn_W1).reshape(EXPERTS, KD, P, HID).transpose(0, 2, 1, 3).reshape(EXPERTS, P, KD * HID)
    w2 = np.asarray(L0_ffn_W2).reshape(EXPERTS, KH, P, D).transpose(0, 2, 1, 3).reshape(EXPERTS, P, KH * D)
    experts = np.concatenate([w1, w2, columns(L0_ffn_ln_g, KD), columns(L0_ffn_ln_b, KD), columns(L0_ffn_b1, KH)], 2)
    arrays = {
        "x": padded(x, ROWS),
        "edges": np.stack([chunks(dst, ROWS), chunks(src, 0), chunks(edge_type_8, 0)], 1),
        "conv": np.asarray(L0_gnn_conv_weights).transpose(2, 0, 1, 3).reshape(D, RELS * D),
        "attn_l": np.asarray(L0_gnn_attn_l).reshape(1, RELS * D),
        "attn_r": np.asarray(L0_gnn_attn_r).reshape(1, RELS * D),
        "bias": np.asarray(L0_gnn_h_bias).reshape(1, D),
        "wr": np.asarray(L0_ffn_Wr),
        "br": np.asarray(L0_ffn_br).reshape(1, EXPERTS),
        "experts": experts.reshape(EXPERTS * P, E_W),
        "b2": np.asarray(L0_ffn_b2),
        "consts": constants(),
    }
    arrays = {name: np.ascontiguousarray(a) for name, a in arrays.items()}
    nc = bacc.Bacc("TRN2", target_bir_lowering=False, num_devices=1)
    ins = {name: nc.dram_tensor(f"in_{name}", a.shape, mybir.dt.from_np(a.dtype), kind="ExternalInput").ap()
           for name, a in arrays.items()}
    out = nc.dram_tensor("out", (ROWS, D), F32, kind="ExternalOutput").ap()
    build(nc, ins, out)
    r = run_bass_kernel_spmd(nc, [{f"in_{name}": a for name, a in arrays.items()}], core_ids=[0])
    return r.results[0]["out"][:N_NODES]
```
